# Optimizing a Trainium2 kernel written in Bass

```python
import numpy as np
import jax
import jax.numpy as jnp

def _softmax(x, axis=-1):
    return jax.nn.softmax(x, axis=axis)

def _gelu(x):
    return jax.nn.gelu(x, approximate=True)

def _silu(x):
    return jax.nn.silu(x)

def _sigmoid(x):
    return jax.nn.sigmoid(x)

def _layernorm(x, axis=-1, eps=1e-05):
    m = jnp.mean(x, axis=axis, keepdims=True)
    v = jnp.var(x, axis=axis, keepdims=True)
    return (x - m) / jnp.sqrt(v + eps)

def _scatter_add(tgt, idx, src, axis=0):
    return tgt.at[idx].add(src)

def _segment_sum(src, seg, n):
    return jax.ops.segment_sum(src, seg, n)
kernel_name = 'mk_adj_ffn_d1_adj_r2_ff921e'

def setup_inputs(seed: int=0):
    np.random.seed(seed)
    _w = jnp.asarray

    def _rec_inputs():
        import jax
        import jax.numpy as jnp
        _gk = jax.random.key(seed)
        x = -0.001547 + 1.001 * jax.random.normal(jax.random.fold_in(_gk, 1), (128, 128, 256), jnp.float32)
        _a = jax.random.bernoulli(jax.random.fold_in(_gk, 2), 0.03125, (128, 128))
        _a = jnp.logical_or(_a, jnp.swapaxes(_a, -1, -2))
        _a = jnp.logical_or(_a, jnp.eye(128, dtype=bool))
        _af = _a.astype(jnp.float32)
        _af = _af * jax.random.uniform(jax.random.fold_in(_gk, 3), (128, 128), jnp.float32, 0.05, 0.237401)
        adj = _af
        return (x, adj)
    x, adj = _rec_inputs()

    def _L0_gnn_setup():
        import jax, jax.numpy as jnp
        import numpy as np
        key = jax.random.key(seed)
        k1, k2, k3, k4 = jax.random.split(key, 4)
        B, D, N = (4, 128, 256)
        scale = 1.0 / np.sqrt(2 * D)
        x = jax.random.normal(k1, (B, D, N), dtype=jnp.float32)
        W1 = jax.random.normal(k2, (D, D), dtype=jnp.float32) * scale
        W2 = jax.random.normal(k3, (D, D), dtype=jnp.float32) * scale
        b = jax.random.normal(k4, (D,), dtype=jnp.float32) * scale
        return {'x': x, 'W1': W1, 'W2': W2, 'b': b}
    _L0_gnn_all = _L0_gnn_setup()
    _L0_gnn_in = {k: v for k, v in _L0_gnn_all.items() if k in ('b',)}
    del _L0_gnn_all

    def _L0_ffn_setup():
        import jax, jax.numpy as jnp
        import numpy as np
        import math
        E, K, CAPF = (8, 2, 1.25)
        D, DFF = (256, 1024)

        def _moe(x, Wr, br, W1, b1, W2, b2):
            orig = x.shape
            d = orig[-1]
            xf = x.reshape(-1, d)
            N = xf.shape[0]
            logits = xf @ Wr + br
            probs = jax.nn.softmax(logits, axis=-1)
            topk_p, topk_i = jax.lax.top_k(probs, K)
            topk_w = topk_p / (jnp.sum(topk_p, axis=-1, keepdims=True) + 1e-09)
            cap = max(1, int(math.ceil(CAPF * float(N * K) / float(E))))
            flat_e = topk_i.reshape(-1)
            flat_w = topk_w.reshape(-1)
            tok = jnp.repeat(jnp.arange(N), K)
            one_hot = jax.nn.one_hot(flat_e, E, dtype=xf.dtype)
            pos = (jnp.cumsum(one_hot, axis=0) - one_hot)[jnp.arange(N * K), flat_e]
            pos = pos.astype(jnp.int32)
            keep = pos < cap
            w_k = jnp.where(keep, flat_w, 0.0)
            sum_w = jnp.zeros((N,), xf.dtype).at[tok].add(w_k)
            w_norm = w_k / (sum_w[tok] + 1e-09)
            slot = flat_e * cap + pos
            slot_safe = jnp.where(keep, slot, E * cap)
            expert_in = jnp.zeros((E * cap, d), xf.dtype).at[slot_safe].set(xf[tok], mode='drop').reshape(E, cap, d)
            h = jax.nn.gelu(jnp.einsum('ecd,edf->ecf', expert_in, W1) + b1[:, None, :], approximate=False)
            expert_out = (jnp.einsum('ecf,efd->ecd', h, W2) + b2[:, None, :]).reshape(E * cap, d)
            contrib = expert_out[jnp.where(keep, slot, 0)]
            y = jnp.zeros((N, d), xf.dtype).at[tok].add(contrib * w_norm[:, None])
            return y.reshape(orig)
        key = jax.random.key(seed)
        ks = jax.random.split(key, 5)
        s = lambda k, sh, sc: jax.random.normal(k, sh, jnp.float32) * sc
        return {'x': jax.random.normal(ks[0], (8, 2048, D), jnp.float32), 'Wr': s(ks[1], (D, E), 1.0 / math.sqrt(D)), 'br': jnp.zeros((E,), jnp.float32), 'W1': s(ks[2], (E, D, DFF), 1.0 / math.sqrt(D)), 'b1': jnp.zeros((E, DFF), jnp.float32), 'W2': s(ks[3], (E, DFF, D), 1.0 / math.sqrt(DFF)), 'b2': jnp.zeros((E, D), jnp.float32)}
    _L0_ffn_all = _L0_ffn_setup()
    _L0_ffn_in = {k: v for k, v in _L0_ffn_all.items() if k in ('Wr', 'br', 'W1', 'b1', 'W2', 'b2')}
    del _L0_ffn_all
    return {'x': x, 'adj': adj, 'L0_gnn_b': _L0_gnn_in['b'], 'L0_ffn_Wr': _L0_ffn_in['Wr'], 'L0_ffn_br': _L0_ffn_in['br'], 'L0_ffn_W1': _L0_ffn_in['W1'], 'L0_ffn_b1': _L0_ffn_in['b1'], 'L0_ffn_W2': _L0_ffn_in['W2'], 'L0_ffn_b2': _L0_ffn_in['b2']}

def reference(x, adj, L0_gnn_b, L0_ffn_Wr, L0_ffn_br, L0_ffn_W1, L0_ffn_b1, L0_ffn_W2, L0_ffn_b2):
    import jax
    import jax.numpy as jnp

    def _L0_gnn_ref(x, W1, W2, b):
        import jax, jax.numpy as jnp
        import numpy as np
        A = jnp.einsum('od,bdn->bon', W1, x)
        C = jnp.einsum('od,bdn->bon', W2, x) + b[None, :, None]
        pre = A[:, :, None, :] + (C - A)[:, :, :, None]
        out = jnp.max(jax.nn.relu(pre), axis=-1)
        return out

    def _L0_ffn_ref(x, Wr, br, W1, b1, W2, b2):
        import jax, jax.numpy as jnp
        import numpy as np
        import math
        E, K, CAPF = (8, 2, 1.25)
        D, DFF = (256, 1024)

        def _moe(x, Wr, br, W1, b1, W2, b2):
            orig = x.shape
            d = orig[-1]
            xf = x.reshape(-1, d)
            N = xf.shape[0]
            logits = xf @ Wr + br
            probs = jax.nn.softmax(logits, axis=-1)
            topk_p, topk_i = jax.lax.top_k(probs, K)
            topk_w = topk_p / (jnp.sum(topk_p, axis=-1, keepdims=True) + 1e-09)
            cap = max(1, int(math.ceil(CAPF * float(N * K) / float(E))))
            flat_e = topk_i.reshape(-1)
            flat_w = topk_w.reshape(-1)
            tok = jnp.repeat(jnp.arange(N), K)
            one_hot = jax.nn.one_hot(flat_e, E, dtype=xf.dtype)
            pos = (jnp.cumsum(one_hot, axis=0) - one_hot)[jnp.arange(N * K), flat_e]
            pos = pos.astype(jnp.int32)
            keep = pos < cap
            w_k = jnp.where(keep, flat_w, 0.0)
            sum_w = jnp.zeros((N,), xf.dtype).at[tok].add(w_k)
            w_norm = w_k / (sum_w[tok] + 1e-09)
            slot = flat_e * cap + pos
            slot_safe = jnp.where(keep, slot, E * cap)
            expert_in = jnp.zeros((E * cap, d), xf.dtype).at[slot_safe].set(xf[tok], mode='drop').reshape(E, cap, d)
            h = jax.nn.gelu(jnp.einsum('ecd,edf->ecf', expert_in, W1) + b1[:, None, :], approximate=False)
            expert_out = (jnp.einsum('ecf,efd->ecd', h, W2) + b2[:, None, :]).reshape(E * cap, d)
            contrib = expert_out[jnp.where(keep, slot, 0)]
            y = jnp.zeros((N, d), xf.dtype).at[tok].add(contrib * w_norm[:, None])
            return y.reshape(orig)
        return _moe(x, Wr, br, W1, b1, W2, b2)
    x = x + _L0_gnn_ref(_layernorm(x, axis=-1), adj, adj, L0_gnn_b)
    x = x + _L0_ffn_ref(_layernorm(x, axis=-1), L0_ffn_Wr, L0_ffn_br, L0_ffn_W1, L0_ffn_b1, L0_ffn_W2, L0_ffn_b2)
    return x

_drawn_inputs = setup_inputs


def setup_inputs(seed=0):
    import zlib

    import numpy as np

    out = dict(_drawn_inputs(seed))
    spreads = {'L0_ffn_br': (0.0, 0.1), 'L0_ffn_b1': (0.0, 0.1), 'L0_ffn_b2': (0.0, 0.1)}
    factors = {}
    for name, (base, spread) in spreads.items():
        noise = np.random.default_rng([zlib.crc32(name.encode()), seed]).standard_normal(out[name].shape)
        drawn = base * np.exp(spread * noise) if base else spread * noise
        out[name] = jnp.asarray(drawn.astype(out[name].dtype))
    for name, factor in factors.items():
        out[name] = (out[name] * factor).astype(out[name].dtype)
    return out
```

```python
from contextlib import ExitStack

import numpy as np

import concourse.bass as bass
from concourse import mybir

F32, F16, I32, U16 = mybir.dt.float32, mybir.dt.float16, mybir.dt.int32, mybir.dt.uint16
ALU = mybir.AluOpType
ACT = mybir.ActivationFunctionType
AX = mybir.AxisListType

P = 128
GRAPHS, NODES, D, DFF, E, K = 128, 128, 256, 1024, 8, 2
TOKENS = GRAPHS * NODES
EPS = 1e-5
CAP = int(np.ceil(1.25 * TOKENS * K / E))

GROUP = 4
NG = GRAPHS // GROUP
SLOTS = 2 * P
NF = TOKENS * K // SLOTS + E - 1
DC, FC = D // P, DFF // P
RTILES = TOKENS // SLOTS + 1
REGION = RTILES * SLOTS
EMPTY_TILE = E * RTILES
ROW = 2 * D + 2 * E + 2
COL_W, COL_TOK = 2 * D, 2 * D + 2 * E

ENTRY_BITS = 7
DEFAULT = (E - 1) * 128 + EMPTY_TILE - (E - 1) * RTILES

XS, WS, HS = 2.0**11, 2.0**8, 2.0**6
LAG = 18
STEPS = NF + LAG + 3
UNROLL = 8


class Step:

    def __init__(self, i, u, reg=None, turns=1):
        self.i, self.u, self.reg = i, u, reg
        self.first = UNROLL * u + i
        self.last = self.first + UNROLL * (turns - 1)

    def at(self, off, limit):
        a, b = (0 <= t - off < limit for t in (self.first, self.last))
        assert a == b
        return a

    def later(self, off, n):
        a, b = (t - off >= n for t in (self.first, self.last))
        assert a == b
        return a

    def val(self, off=0, div=1, mult=1, plus=0):
        base = mult * ((self.first - off) // div) + plus
        return base if self.reg is None else self.reg * (UNROLL // div * mult) + base

    def slot(self, off, n):
        return (self.i - off) % n


def steps(eng, body):
    def run(u0, u1):
        for u in range(u0, u1):
            for i in range(UNROLL):
                if UNROLL * u + i < STEPS:
                    body(Step(i, u))

    def loop(u0, u1):
        with eng.Fori(0, u1 - u0) as reg:
            for i in range(UNROLL):
                body(Step(i, u0, reg, u1 - u0))

    full = (LAG + 3) // UNROLL + 1
    drain = GRAPHS // UNROLL
    run(0, full)
    loop(full, drain - 1)
    run(drain - 1, STEPS // UNROLL + 1)


def build(nc, x, adj, gnn_b, Wr, br, W1, b1, W2, b2, out):
    x_rows = x.rearrange("b p c -> (b p) c")
    out_rows = out.rearrange("b p c -> (b p) c")
    out_words = out_rows.bitcast(I32)
    records = nc.dram_tensor("records", [(EMPTY_TILE + 1) * SLOTS, ROW], U16, kind="Internal").ap()

    with ExitStack() as ctx:
        def sb(name, shape, dt):
            return ctx.enter_context(nc.sbuf_tensor(name, shape, dt))

        def sem(name):
            return ctx.enter_context(nc.semaphore(name))

        w_all = sb("w_all", [P, E, 4, DC * DFF], F16)
        b1_col = sb("b1_col", [P, E * FC], F32)
        b2_bc = sb("b2_bc", [P, E, D], F32)
        hidden = sb("hidden", [P, 2, 2, FC * SLOTS], F16)
        stage = hidden[:].bitcast(F32).rearrange("p a b c -> p a (b c)")
        h32 = sb("h32", [P, 2, 2 * SLOTS], F32)
        rows = sb("rows", [P, 2, 2, ROW], U16)
        xt = sb("xt", [P, 2, 2, 2 * SLOTS], F16)
        tok = sb("tok", [P, 4, 2], I32)
        wsel = sb("wsel", [P, 4, 2], F32)
        old = sb("old", [P, 2, 2, D], F32)
        res = sb("res", [P, 2, 2, D], F32)
        xin = sb("xin", [P, 8, D], F32)
        xs = sb("xs", [P, 2, D], F32)
        rec = sb("rec", [P, 8, ROW], U16)
        xta = sb("xta", [P, 2, 4 * P], F16)
        stats = sb("stats", [P, 4, 6], F32)
        mv = sb("mv", [P, 4, 2], F32)
        var_eps = sb("var_eps", [P, 2], F32)
        minus_half = sb("minus_half", [P, 1], F32)
        rstd = sb("rstd", [P, 4], F32)
        amax = sb("amax", [P, 3], F32)
        ident = sb("ident", [P, P], F16)
        identf = sb("identf", [P, P], F32)
        before = sb("before", [P, P], F16)
        beforef = sb("beforef", [E, E], F32)
        ones = sb("ones", [P, P], F16)
        onesf = sb("onesf", [E, E], F32)
        iota_i = sb("iota_i", [P, 1 + NF], I32)
        rank = sb("rank", [P, E], F32)
        region_row = sb("region_row", [P, E], F32)
        entry_no = sb("entry_no", [E, NF], F32)
        entry_base = sb("entry_base", [E, 1], F32)
        tok_no = sb("tok_no", [P, GROUP], F32)
        pad_rec = sb("pad_rec", [P, ROW], U16)
        adj_in = sb("adj_in", [P, P], F32)
        adj_t = sb("adj_t", [P, 2, P], F16)
        wr_in = sb("wr_in", [P, DC, E], F32)
        wr16 = sb("wr16", [P, DC, 2 * E], F16)
        br_bc = sb("br_bc", [P, E], F32)
        gb_col = sb("gb_col", [P, 1], F32)
        lg = sb("lg", [P, GROUP, E], F32)
        r = {n: sb("r_" + n, [P, GROUP, E], F32) for n in (
            "L", "eq", "rk", "oh1", "L2", "oh2", "D", "E", "W", "pos", "keep", "v1", "v2")}
        s = {n: sb("s_" + n, [P, GROUP], F32) for n in ("m1", "r1", "m2", "r2", "a", "b", "c", "d")}
        chosen = sb("chosen", [P, GROUP + 1, E], F16)
        dest = sb("dest", [P, 2, K, GROUP], I32)
        count = sb("count", [P, E], F32)
        ev_cc = sb("ev_cc", [E, E], F32)
        ev_i = sb("ev_i", [E, 2], I32)
        ev = sb("ev", [E, 6], F32)
        ev_a = sb("ev_a", [E, NF], F32)
        ev_b = sb("ev_b", [E, NF], F32)
        entries = sb("entries", [E, NF], F16)
        entry_t = sb("entry_t", [1, NF], I32)
        expert_t = sb("expert_t", [1, NF], I32)
        rowtile_t = sb("rowtile_t", [1, NF], I32)
        count_t = sb("count_t", [1, E], I32)

        ps1 = [ctx.enter_context(nc.psum_tensor(f"ps1_{k}", [P, 2 * SLOTS], F32)) for k in range(4)]
        psy = ctx.enter_context(nc.psum_tensor("psy", [P, 2, D], F32))
        ps_xt = ctx.enter_context(nc.psum_tensor("ps_xt", [P, 2, 2 * SLOTS], F16))
        psa = ctx.enter_context(nc.psum_tensor("psa", [P, 512], F32))
        ps_xta = psa[:, 0:2 * P].bitcast(F16)
        ps_lg = psa[:, 0:2 * E]
        ps_gnn = psa[:, 2 * P:2 * P + D]
        pss = ctx.enter_context(nc.psum_tensor("pss", [P, 512], F32))
        ps_pos = pss[:, 128:128 + (GROUP + 1) * E].rearrange("p (t e) -> p t e", e=E)
        ps_first = pss[0:E, 176:177]
        ps_list = pss[0:1, 192:192 + NF]

        const_in = sem("const_in")
        x_in = [sem(f"x_in{k}") for k in range(4)]
        w_in = [sem(f"w_in{k}") for k in range(2)]
        rows_in = [sem(f"rows_in{k}") for k in range(2)]
        old_in = [sem(f"old_in{k}") for k in range(2)]
        init_out = [sem(f"init_out{k}") for k in range(4)]
        scattered = [sem(f"scattered{k}") for k in range(8)]
        added = [sem(f"added{k}") for k in range(2)]
        empty_out = sem("empty_out")
        pads_out = sem("pads_out")
        pool_set = sem("pool_set")
        dve_set = sem("dve_set")
        pe_set = sem("pe_set")
        act_set = sem("act_set")
        w_scaled = sem("w_scaled")
        w_hi = sem("w_hi")
        w_lo = sem("w_lo")
        stats_done = sem("stats_done")
        stats_mid = sem("stats_mid")
        var_done = sem("var_done")
        rstd_done = sem("rstd_done")
        xs_done = sem("xs_done")
        rec_hi = sem("rec_hi")
        rec_done = sem("rec_done")
        xta_psum = sem("xta_psum")
        xta_done = sem("xta_done")
        gnn_done = sem("gnn_done")
        amax_done = sem("amax_done")
        amax_mid = sem("amax_mid")
        init_done = sem("init_done")
        diff_done = sem("diff_done")
        chosen_done = sem("chosen_done")
        exp_done = sem("exp_done")
        pos_done = sem("pos_done")
        pos_read = sem("pos_read")
        routed = sem("routed")
        new_tiles = sem("new_tiles")
        first_done = sem("first_done")
        entries_done = sem("entries_done")
        list_psum = sem("list_psum")
        list_done = sem("list_done")
        counts_done = sem("counts_done")
        norm_done = sem("norm_done")
        chain = sem("chain")
        tab_sem = sem("tab_sem")
        meta_done = sem("meta_done")
        xt_psum = sem("xt_psum")
        xt_done = sem("xt_done")
        h_psum = sem("h_psum")
        gelu_done = sem("gelu_done")
        h_hi = sem("h_hi")
        h_done = sem("h_done")
        y_psum = sem("y_psum")
        y_read = sem("y_read")
        res_done = sem("res_done")

        waits_alone = {eng.engine: sem(f"waits_alone_{n}") for n, eng in (
            ("pool", nc.gpsimd), ("dve", nc.vector), ("pe", nc.tensor))}

        block = ctx.enter_context(nc.Block())

        def table(t, st, off, n=1):
            return t[0:1, bass.DynSlice(st.val(off), n)] if st.reg is not None else t[0:1, st.val(off):st.val(off) + n]

        def load_expert(eng, st, off):
            return eng.value_load(table(expert_t, st, off), min_val=0, max_val=E - 1)

        def wait_alone(eng, semaphore, value):
            eng.wait_ge(semaphore, value)
            eng.sem_inc(waits_alone[eng.engine], 1)

        def min_list(st, off):
            return NG - 1 if st.later(off, GROUP * (NG - 2)) else st.val(off, GROUP, 1, 1)

        @block.sync
        def _(sp):
            def x_load(st, off):
                pair = st.slot(off, 8) // 2
                src = x_rows.rearrange("(t p) c -> p t c", p=P)
                t0 = st.val(off)
                tiles = src[:, bass.DynSlice(t0, 2), :] if st.reg is not None else src[:, t0:t0 + 2, :]
                sp.dma_start(xin[:, 2 * pair:2 * pair + 2, :], tiles).then_inc(x_in[pair], 16)

            def w_load(k):
                if k >= 2:
                    sp.wait_ge(w_hi, k - 1)
                    sp.wait_ge(w_lo, k - 1)
                src = (W1, W2)[k % 2][k // 2].rearrange("(c p) f -> p c f", p=P)
                c = (DC, FC)[k % 2]
                sp.dma_start(stage[:, k % 2, :].rearrange("p (c f) -> p c f", c=c), src).then_inc(w_in[k % 2], 16)

            x_load(Step(0, 0), 0)
            x_load(Step(2, 0), 0)
            sp.dma_start(adj_in[:], adj).then_inc(const_in, 16)
            sp.dma_start(wr_in[:], Wr.rearrange("(c p) e -> p c e", p=P)).then_inc(const_in, 16)
            sp.dma_start(br_bc[:], br.rearrange("(a e) -> a e", a=1).broadcast_to([P, E])).then_inc(const_in, 16)
            sp.dma_start(gb_col[:], gnn_b.rearrange("(p a) -> p a", a=1)).then_inc(const_in, 16)
            sp.dma_start(h32[0:E * FC, 0, 0:P], b1.rearrange("e (c p) -> (e c) p", p=P)).then_inc(const_in, 16)
            sp.dma_start(b2_bc[:], b2.rearrange("(a e) d -> a e d", a=1).broadcast_to([P, E, D])).then_inc(const_in, 16)
            sp.wait_ge(pool_set, 4)
            for h in range(2):
                r0 = EMPTY_TILE * SLOTS + h * P
                sp.dma_start(records[r0:r0 + P, :], pad_rec[:]).then_inc(empty_out, 16)

            def body(st):
                if st.reg is None and st.first < 2 * E:
                    w_load(st.first)
                off = LAG - 2
                if st.at(off, NF):
                    if st.slot(off, 4) == 0:
                        m = (st.first - off) // GROUP
                        if st.later(off, GROUP * (NG - 2)):
                            if st.first - off == GROUP * (NG - 2):
                                sp.wait_ge(list_done, NG - 1)
                                sp.wait_ge(pads_out, 16 * 2 * E)
                                sp.wait_ge(empty_out, 32)
                        else:
                            sp.wait_ge(list_done, st.val(off, GROUP, 1, 1))
                            for k in range(GROUP):
                                sp.wait_ge(scattered[st.slot(off - 2 * GROUP, 8) + k],
                                           st.val(off - 2 * GROUP, 8, 32, 32))
                    if st.later(off, 2):
                        sp.wait_ge(xt_psum, st.val(off, plus=-1))
                        sp.wait_ge(meta_done, st.val(off, plus=-1))
                    q = sp.value_load(table(rowtile_t, st, off), min_val=0, max_val=EMPTY_TILE)
                    src = records.rearrange("(n h p) c -> n p h c", h=2, p=P)[bass.DynSlice(q, 1)]
                    slot = st.slot(off, 2)
                    sp.dma_start(rows[:, slot], src.rearrange("n p h c -> p (n h) c")).then_inc(rows_in[slot], 16)
                if st.i % 2 == 0 and st.at(-4, GRAPHS):
                    if st.later(4, 0):
                        for k in range(2):
                            sp.wait_ge(init_out[st.slot(4, 4) + k], st.val(4, 4, 16, 16))
                    x_load(st, -4)
                if st.at(1, GRAPHS):
                    sp.wait_ge(init_done, st.val(0))
                    src = xin[:, st.slot(1, 8), :]
                    dst = out_rows.rearrange("(t p) c -> t p c", p=P)
                    t0 = st.val(1)
                    dst = dst[bass.DynSlice(t0, 1)].rearrange("t p c -> (t p) c") if st.reg is not None else dst[t0]
                    sp.dma_start(dst, src).then_inc(init_out[st.slot(1, 4)], 16)
                if st.reg is None and st.first == GRAPHS + 2:
                    sp.wait_ge(counts_done, 1)
                    for e in range(E):
                        n = sp.value_load(count_t[0:1, e:e + 1], min_val=0, max_val=TOKENS)
                        for h in range(2):
                            dst = records[bass.DynSlice(n + (e * REGION + h * P), P), :]
                            sp.dma_start(dst, pad_rec[:]).then_inc(pads_out, 16)

            steps(sp, body)
            for k in range(2):
                sp.wait_ge(added[k], 32 * ((NF + 1 - k) // 2))

        @block.gpsimd
        def _(pool):
            pool.memset(ident[:], 0.0)
            pool.memset(identf[:], 0.0)
            pool.memset(before[:], 1.0)
            pool.memset(pad_rec[:], 0)
            pool.memset(minus_half[:], -0.5)
            pool.memset(beforef[:], 1.0)
            pool.memset(onesf[:], 1.0)
            pool.memset(ones[:], 1.0)
            pool.memset(old[:], 0.0).then_inc(pool_set, 1)
            pool.wait_ge(pool_set, 1)
            pool.affine_select(out=ident[:], in_=ident[:], compare_op=ALU.not_equal, fill=1.0, base=0,
                               pattern=[[-1, P]], channel_multiplier=1)
            pool.affine_select(out=identf[:], in_=identf[:], compare_op=ALU.not_equal, fill=1.0, base=0,
                               pattern=[[-1, P]], channel_multiplier=1)
            pool.affine_select(out=before[:], in_=before[:], compare_op=ALU.is_gt, fill=0.0, base=0,
                               pattern=[[1, P]], channel_multiplier=-1)
            pool.affine_select(out=beforef[:], in_=beforef[:], compare_op=ALU.is_gt, fill=0.0, base=0,
                               pattern=[[1, E]], channel_multiplier=-1).then_inc(pool_set, 1)
            pool.iota(iota_i[:, 0:1], pattern=[[0, 1]], base=0, channel_multiplier=1)
            pool.iota(iota_i[:, 1:1 + NF], pattern=[[1, NF]], base=0, channel_multiplier=0).then_inc(pool_set, 1)
            pool.memset(pad_rec[:, COL_TOK:ROW].bitcast(I32), TOKENS).then_inc(pool_set, 1)

            def inverse_deviation(st, off):
                slot = st.slot(off, 4)
                wait_alone(pool, stats_done, st.val(off, plus=1))
                two = st.slot(off, 2)
                pool.tensor_scalar(var_eps[:, two:two + 1], mv[:, slot, 1:2], EPS, None, ALU.add).then_inc(var_done, 1)
                pool.wait_ge(var_done, st.val(off, plus=1))
                pool.tensor_tensor(rstd[:, slot:slot + 1], var_eps[:, two:two + 1], minus_half[:], ALU.pow).then_inc(rstd_done, 1)

            def records_out(st, off, par):
                slot = st.slot(off, 8)
                for k in range(K):
                    pool.indirect_dma_start(
                        out=records, out_offset=bass.IndirectOffsetOnAxis(
                            ap=dest[:, par, k, slot % GROUP:slot % GROUP + 1], axis=0),
                        in_=rec[:, slot, :], in_offset=None).then_inc(scattered[slot], 16)

            def body(st):
                off = LAG + 2
                if st.at(off, NF):
                    slot = st.slot(off, 2)
                    wait_alone(pool, res_done, st.val(off, plus=1))
                    for h in range(2):
                        pool.indirect_dma_start(
                            out=out_rows, out_offset=bass.IndirectOffsetOnAxis(
                                ap=tok[:, st.slot(off, 4), h:h + 1], axis=0),
                            in_=res[:, slot, h, :], in_offset=None,
                            bounds_check=TOKENS - 1, oob_is_err=False).then_inc(added[slot], 16)
                if st.i % GROUP >= 2:
                    first = st.i % GROUP * 2 - 4
                    goff = GROUP + st.i % 4 - first
                    if st.at(goff, GRAPHS):
                        if first == 0:
                            wait_alone(pool, routed, st.val(goff, GROUP, 1, 1))
                        records_out(st, goff, st.slot(goff, 8) // GROUP)
                        records_out(st, goff - 1, st.slot(goff, 8) // GROUP)
                off = LAG + 1
                if st.at(off, NF):
                    slot = st.slot(off, 2)
                    wait_alone(pool, meta_done, st.val(off, plus=1))
                    if st.later(off, 1):
                        wait_alone(pool, added[1 - slot], st.val(off + 1, 2, 32, 32))
                    if st.slot(off, 4) == 0 and not st.later(off, GROUP * (NG - 2)):
                        for k in range(4):
                            wait_alone(pool, init_out[k], st.val(off - 2 * GROUP, GROUP, 16, 16))
                    for h in range(2):
                        pool.indirect_dma_start(
                            out=old[:, slot, h, :].bitcast(I32), out_offset=None, in_=out_words,
                            in_offset=bass.IndirectOffsetOnAxis(ap=tok[:, st.slot(off, 4), h:h + 1], axis=0),
                            bounds_check=TOKENS - 1, oob_is_err=False).then_inc(old_in[slot], 16)
                if st.at(-3, GRAPHS):
                    inverse_deviation(st, -3)
                if st.reg is None and st.first < 2 * E:
                    k = st.first
                    pool.wait_ge(w_hi, k + 1)
                    pool.tensor_tensor(w_all[:, k // 2, 2 * (k % 2) + 1, :], stage[:, k % 2, :],
                                       w_all[:, k // 2, 2 * (k % 2), :], ALU.subtract).then_inc(w_lo, 1)

            for t in range(3):
                inverse_deviation(Step(t, 0), 0)
            steps(pool, body)

        @block.scalar
        def _(act):
            act.wait_ge(pe_set, 1)
            act.activation(adj_t[:, 0, :], ps1[0][:, 0:P], ACT.Copy, scale=WS)
            act.activation(b1_col[:], ps1[1][:, 0:E * FC], ACT.Copy).then_inc(act_set, 1)

            def body(st):
                if st.reg is None and st.first < 2 * E:
                    k = st.first
                    act.wait_ge(w_in[k % 2], 16 * (k // 2 + 1))
                    act.activation(stage[:, k % 2, :], stage[:, k % 2, :], ACT.Copy, scale=WS).then_inc(w_scaled, 1)
                    act.wait_ge(w_scaled, k + 1)
                    act.activation(w_all[:, k // 2, 2 * (k % 2), :], stage[:, k % 2, :], ACT.Copy).then_inc(w_hi, 1)
                if st.at(0, GRAPHS):
                    act.wait_ge(xta_psum, st.val(0, plus=1))
                    if st.later(0, 2):
                        act.wait_ge(gnn_done, st.val(0, plus=-1))
                    act.activation(xta[:, st.slot(0, 2), :], ps_xta, ACT.Copy).then_inc(xta_done, 1)
                if st.i % GROUP == 0 and st.at(GROUP, GRAPHS):
                    act.wait_ge(diff_done, st.val(GROUP, GROUP, 1, 1))
                    if st.later(GROUP, GROUP):
                        act.wait_ge(routed, st.val(GROUP, GROUP))
                    act.activation(r["E"][:], r["D"][:], ACT.Exp).then_inc(exp_done, 1)
                off = LAG
                if st.at(off, NF):
                    e = load_expert(act, st, off)
                    par = st.slot(off, 2)

                    def gelu(q):
                        act.wait_ge(h_psum, st.val(off, 1, FC, 2 * q + 2))
                        if st.later(off, 1) or q >= 2:
                            act.wait_ge(h_done, st.val(off, 1, FC // 2, q - 1))
                        for c in (2 * q, 2 * q + 1):
                            act.activation(h32[:, q % 2, c % 2 * SLOTS:(c % 2 + 1) * SLOTS],
                                           ps1[q][:, c % 2 * SLOTS:(c % 2 + 1) * SLOTS], ACT.Gelu,
                                           bias=b1_col[:, bass.DynSlice(e * FC + c, 1)],
                                           scale=1 / (XS * WS)).then_inc(gelu_done, 1)

                    def hi(q):
                        act.wait_ge(gelu_done, st.val(off, 1, FC, 2 * q + 2))
                        if q == 0 and st.later(off, 2):
                            act.wait_ge(y_psum, st.val(off, plus=-1))
                        if q == 0 and not st.later(off, 2):
                            act.wait_ge(w_hi, 2 * E)
                            act.wait_ge(w_lo, 2 * E)
                        act.activation(hidden[:, par, 0, q * 2 * SLOTS:(q + 1) * 2 * SLOTS], h32[:, q % 2, :],
                                       ACT.Copy, scale=HS).then_inc(h_hi, 1)

                    gelu(0)
                    gelu(1)
                    hi(0)
                    hi(1)
                    gelu(2)
                    gelu(3)
                    hi(2)
                    hi(3)
                off = LAG - 1
                if st.at(off, NF):
                    act.wait_ge(xt_psum, st.val(off, plus=1))
                    if st.later(off, 2):
                        act.wait_ge(h_psum, st.val(off, 1, FC, -FC))
                    act.activation(xt[:, st.slot(off, 2)], ps_xt[:], ACT.Copy).then_inc(xt_done, 1)

            steps(act, body)

        @block.vector
        def _(dve):
            links = [0]

            def link(ins):
                links[0] += 1
                ins.then_inc(dve_set, 1)
                dve.wait_ge(dve_set, links[0])

            def do_stats(st, off):
                pair = st.slot(off, 8) // 2
                dve.wait_ge(x_in[pair], st.val(off, 8, 16, 16))
                dve.bn_stats(stats[:, st.slot(off, 4), :], xin[:, st.slot(off, 8), :]).then_inc(stats_mid, 1)
                wait_alone(dve, stats_mid, st.val(off, plus=1))
                dve.bn_aggr(mv[:, st.slot(off, 4), :], stats[:, st.slot(off, 4), :]).then_inc(stats_done, 1)

            def do_xs(st, off):
                slot = st.slot(off, 4)
                dve.wait_ge(rstd_done, st.val(off, plus=1))
                dve.tensor_scalar(xs[:, st.slot(off, 2), :], xin[:, st.slot(off, 8), :], mv[:, slot, 0:1], rstd[:, slot:slot + 1],
                                  ALU.subtract, ALU.mult).then_inc(xs_done, 1)

            def do_rec_hi(st, off):
                slot = st.slot(off, 8)
                if st.later(off, 8):
                    dve.wait_ge(scattered[slot], st.val(off, 8, 32))
                dve.wait_ge(xs_done, st.val(off, plus=1))
                dve.tensor_scalar(rec[:, slot, 0:D].bitcast(F16), xs[:, st.slot(off, 2), :], XS, None, ALU.mult).then_inc(rec_hi, 1)

            def do_rec_lo(st, off):
                slot = st.slot(off, 8)
                dve.wait_ge(rec_hi, st.val(off, plus=1))
                dve.scalar_tensor_tensor(rec[:, slot, D:2 * D].bitcast(F16), xs[:, st.slot(off, 2), :], XS, rec[:, slot, 0:D].bitcast(F16),
                                         ALU.mult, ALU.subtract).then_inc(rec_done, 1)

            for t in range(3):
                do_stats(Step(t, 0), 0)
            dve.wait_ge(pool_set, 4)
            dve.memset(count[:], 0.0)
            dve.memset(chosen[:], 0.0)
            dve.memset(entries[:], 0.0)
            dve.memset(ev[:], 0.0)
            dve.tensor_scalar(rank[:], iota_i[:, 1:1 + E], -1.0, float(E), ALU.mult, ALU.add)
            dve.tensor_scalar(region_row[:], iota_i[:, 1:1 + E], float(REGION), None, ALU.mult)
            dve.tensor_copy(entry_no[:], iota_i[0:E, 1:1 + NF])
            dve.tensor_scalar(entry_base[:], iota_i[0:E, 0:1], 128.0, -float(DEFAULT), ALU.mult, ALU.add)
            dve.tensor_scalar(tok_no[:], iota_i[:, 1:1 + GROUP], float(P), None, ALU.mult)
            dve.wait_ge(const_in, 16 * 6)
            link(dve.tensor_scalar(wr16[:, :, 0:E], wr_in[:], WS, None, ALU.mult))
            dve.scalar_tensor_tensor(wr16[:, :, E:2 * E], wr_in[:], WS, wr16[:, :, 0:E], ALU.mult, ALU.subtract)
            dve.tensor_copy(s["a"][:, 0:1], iota_i[:, 0:1])
            dve.wait_ge(act_set, 1)
            link(dve.scalar_tensor_tensor(adj_t[:, 1, :], ps1[0][:, 0:P], WS, adj_t[:, 0, :], ALU.mult, ALU.subtract))
            link(dve.tensor_scalar(tok_no[:], tok_no[:], s["a"][:, 0:1], None, ALU.add))
            setup_links = links[0]
            do_xs(Step(0, 0), 0)
            do_rec_hi(Step(0, 0), 0)
            do_rec_lo(Step(0, 0), 0)

            TOP, SOFT, PLACE, FULL, REST, NEW = 12, 7, 1, 5, 7, 6
            PER_GROUP = TOP + SOFT + PLACE + FULL + REST + NEW

            class Chain:

                def __init__(self, st, off, start):
                    self.st, self.off, self.start, self.k = st, off, start, 0

                def __call__(self, ins):
                    self.k += 1
                    ins.then_inc(chain, 1)
                    dve.wait_ge(chain, self.st.val(self.off, GROUP, PER_GROUP, self.start + self.k))

            def bc(a):
                return a[:, :, None].broadcast_to([P, GROUP, E])

            def over_tiles(a):
                return a[:, None, :].broadcast_to([P, GROUP, E])

            def top(link, values, m, rk, onehot):
                link(dve.tensor_reduce(s[m][:], values[:], AX.X, ALU.max))
                link(dve.tensor_tensor(r["eq"][:], values[:], bc(s[m]), ALU.is_equal))
                link(dve.tensor_tensor(r["rk"][:], r["eq"][:], over_tiles(rank), ALU.mult))
                link(dve.tensor_reduce(s[rk][:], r["rk"][:], AX.X, ALU.max))
                link(dve.tensor_tensor(onehot[:], r["rk"][:], bc(s[rk]), ALU.is_equal))

            def route_top(st, off):
                link = Chain(st, off, 0)
                dve.wait_ge(amax_done, st.val(off, GROUP, GROUP, GROUP))
                link(dve.scalar_tensor_tensor(r["L"][:], lg[:], 1 / (XS * WS), over_tiles(br_bc), ALU.mult, ALU.add))
                top(link, r["L"], "m1", "r1", r["oh1"])
                dve.tensor_tensor(r["D"][:], r["L"][:], bc(s["m1"]), ALU.subtract).then_inc(diff_done, 1)
                link(dve.scalar_tensor_tensor(r["L2"][:], r["oh1"][:], -1e30, r["L"][:], ALU.mult, ALU.add))
                top(link, r["L2"], "m2", "r2", r["oh2"])
                if st.later(off, GROUP):
                    dve.wait_ge(pos_done, st.val(off, GROUP))
                dve.tensor_tensor(chosen[:, 0:GROUP, :], r["oh1"][:], r["oh2"][:], ALU.add).then_inc(chosen_done, 1)
                dve.wait_ge(chosen_done, st.val(off, GROUP, 1, 1))
                assert link.k == TOP

            def softmax(st, off):
                link = Chain(st, off, TOP)
                dve.wait_ge(exp_done, st.val(off, GROUP, 1, 1))
                dve.tensor_tensor(r["W"][:], r["E"][:], chosen[:, 0:GROUP, :], ALU.mult)
                link(dve.tensor_reduce(s["a"][:], r["E"][:], AX.X, ALU.add))
                link(dve.reciprocal(s["b"][:], s["a"][:]))
                link(dve.tensor_tensor(r["W"][:], r["W"][:], bc(s["b"]), ALU.mult))
                link(dve.tensor_reduce(s["a"][:], r["W"][:], AX.X, ALU.add))
                link(dve.tensor_scalar(s["a"][:], s["a"][:], 1e-9, None, ALU.add))
                link(dve.reciprocal(s["b"][:], s["a"][:]))
                link(dve.tensor_tensor(r["W"][:], r["W"][:], bc(s["b"]), ALU.mult))
                assert link.k == SOFT

            def places(st, off):
                link = Chain(st, off, TOP + SOFT)
                dve.wait_ge(pos_done, st.val(off, GROUP, 1, 1))
                link(dve.tensor_tensor(r["pos"][:], ps_pos[:, 0:GROUP, :], over_tiles(count), ALU.add))
                dve.tensor_tensor(count[:], count[:], ps_pos[:, GROUP, :], ALU.add).then_inc(pos_read, 1)
                dve.wait_ge(pos_read, st.val(off, GROUP, 1, 1))

            def route_rest(st, off):
                link = Chain(st, off, TOP + SOFT + PLACE + FULL)
                par = st.slot(off, 8) // GROUP
                recs = rec[:, GROUP * par:GROUP * par + GROUP, :]
                link(dve.tensor_scalar(r["keep"][:], r["pos"][:], float(CAP), None, ALU.is_lt))
                link(dve.tensor_tensor(r["W"][:], r["W"][:], r["keep"][:], ALU.mult))
                link(dve.tensor_reduce(s["a"][:], r["W"][:], AX.X, ALU.add))
                dve.tensor_scalar(s["a"][:], s["a"][:], 1e-9, None, ALU.add).then_inc(norm_done, 1)
                link(dve.tensor_tensor(r["pos"][:], r["pos"][:], over_tiles(region_row), ALU.add))
                dve.wait_ge(norm_done, st.val(off, GROUP, 1, 1))
                link(dve.reciprocal(s["b"][:], s["a"][:]))
                dve.tensor_tensor(recs[:, :, COL_W:COL_TOK].bitcast(F32), r["W"][:], bc(s["b"]), ALU.mult)
                dve.tensor_copy(recs[:, :, COL_TOK:ROW].bitcast(I32), tok_no[:][:, :, None])
                dve.tensor_tensor(r["v1"][:], r["oh1"][:], r["pos"][:], ALU.mult)
                link(dve.tensor_tensor(r["v2"][:], r["oh2"][:], r["pos"][:], ALU.mult))
                dve.tensor_scalar(tok_no[:], tok_no[:], float(GROUP * P), None, ALU.add)
                dve.tensor_reduce(s["c"][:], r["v1"][:], AX.X, ALU.add)
                link(dve.tensor_reduce(s["d"][:], r["v2"][:], AX.X, ALU.add))
                dve.tensor_copy(dest[:, par, 0, :], s["c"][:])
                dve.tensor_copy(dest[:, par, 1, :], s["d"][:]).then_inc(routed, 1)
                dve.wait_ge(routed, st.val(off, GROUP, 1, 1))
                assert link.k == REST

            def full_tiles(link, up):
                link(dve.tensor_tensor(ev_cc[:], count[0:E, :], identf[0:E, 0:E], ALU.mult))
                link(dve.tensor_reduce(ev[:, 5:6], ev_cc[:], AX.X, ALU.add))
                link(dve.tensor_scalar(ev_i[:, 0:1], ev[:, 5:6], float(up), None, ALU.add))
                link(dve.tensor_scalar(ev_i[:, 1:2], ev_i[:, 0:1], 8, None, ALU.logical_shift_right))
                link(dve.tensor_copy(ev[:, 1:2], ev_i[:, 1:2]))
                dve.tensor_tensor(ev[:, 2:3], ev[:, 1:2], ev[:, 0:1], ALU.subtract).then_inc(new_tiles, 1)

            def list_new(link):
                link(dve.tensor_copy(ev[:, 3:4], ps_first))
                link(dve.tensor_tensor(ev[:, 4:5], ev[:, 3:4], ev[:, 2:3], ALU.add))
                link(dve.scalar_tensor_tensor(ev[:, 5:6], ev[:, 0:1], entry_base[:, 0:1], ev[:, 3:4],
                                              ALU.add, ALU.subtract))
                dve.tensor_copy(ev[:, 0:1], ev[:, 1:2])
                link(dve.tensor_scalar(ev_a[:], entry_no[:], ev[:, 3:4], None, ALU.is_ge))
                link(dve.scalar_tensor_tensor(ev_b[:], entry_no[:], ev[:, 4:5], ev_a[:], ALU.is_lt, ALU.mult))
                link(dve.scalar_tensor_tensor(ev_a[:], entry_no[:], ev[:, 5:6], ev_b[:], ALU.add, ALU.mult))
                dve.tensor_tensor(entries[:], entries[:], ev_a[:], ALU.add).then_inc(entries_done, 1)

            def tables(link, window, n):
                def win(t):
                    return t[0:1, window]
                link(dve.tensor_scalar(win(entry_t), ps_list[:, window], float(DEFAULT), None, ALU.add))
                link(dve.tensor_scalar(win(expert_t), win(entry_t), ENTRY_BITS, None, ALU.logical_shift_right))
                dve.scalar_tensor_tensor(win(rowtile_t), win(expert_t), float(RTILES - 128), win(entry_t),
                                         ALU.mult, ALU.add).then_inc(list_done, 1)

            def routing_between(st):
                part = st.i % GROUP
                if part == 0 and st.at(GROUP, GRAPHS):
                    softmax(st, GROUP)
                if part == 1 and st.at(GROUP + 1, GRAPHS):
                    route_rest(st, GROUP + 1)
                if part == 2 and st.at(GROUP + 2, GRAPHS):
                    dve.wait_ge(first_done, st.val(GROUP + 2, GROUP, 1, 1))
                    if st.later(GROUP + 2, GROUP):
                        dve.wait_ge(list_psum, st.val(GROUP + 2, GROUP))
                    list_new(Chain(st, GROUP + 2, TOP + SOFT + PLACE + FULL + REST))
                if part == 3 and st.at(GROUP + 3, GRAPHS) and st.later(GROUP + 3, 2 * GROUP):
                    dve.wait_ge(list_psum, st.val(GROUP + 3, GROUP, 1, 1))
                    first = st.val(3 * GROUP + 3, GROUP, GROUP)
                    tables(Tables(st), bass.DynSlice(first, GROUP) if st.reg is not None
                           else slice(first, first + GROUP), GROUP)

            def routing(st):
                part = st.i % GROUP
                if part == 3 and st.at(3, GRAPHS):
                    route_top(st, 3)
                if part == 0 and st.at(GROUP, GRAPHS):
                    places(st, GROUP)
                    if st.later(GROUP, GROUP):
                        dve.wait_ge(entries_done, st.val(GROUP, GROUP))
                    full_tiles(Chain(st, GROUP, TOP + SOFT + PLACE), 0)
                if st.reg is None:
                    fin = lambda ins: (ins.then_inc(dve_set, 1), last.__setitem__(0, last[0] + 1),
                                       dve.wait_ge(dve_set, last[0]))
                    if st.first == GRAPHS + 1:
                        dve.tensor_copy(count_t[:], count[0:1, :]).then_inc(counts_done, 1)
                    if st.first == GRAPHS + GROUP:
                        dve.wait_ge(entries_done, NG)
                        full_tiles(fin, SLOTS - 1)
                    if st.first == GRAPHS + GROUP + 1:
                        dve.wait_ge(first_done, NG + 1)
                        dve.wait_ge(list_psum, NG)
                        list_new(fin)
                    if st.first == GRAPHS + GROUP + 2:
                        dve.wait_ge(list_psum, NG + 1)
                        tables(fin, slice(GROUP * (NG - 2), NF), NF - GROUP * (NG - 2))

            last = [setup_links]

            class Tables:
                def __init__(self, st):
                    self.st, self.k = st, 0

                def __call__(self, ins):
                    self.k += 1
                    ins.then_inc(tab_sem, 1)
                    dve.wait_ge(tab_sem, self.st.val(3 * GROUP + 3, GROUP, 2, self.k))

            def body(st):
                nxt = st.at(-1, GRAPHS)
                if nxt:
                    do_xs(st, -1)
                off = LAG + 2
                yt = st.at(off, NF)
                if yt:
                    slot = st.slot(off, 2)
                    e = load_expert(dve, st, off)
                    if st.later(off, 2):
                        dve.wait_ge(added[slot], st.val(off, 2, 32))
                    dve.wait_ge(y_psum, st.val(off, plus=1))
                    dve.scalar_tensor_tensor(res[:, slot], psy[:], 1 / (HS * WS),
                                             b2_bc[:, bass.DynSlice(e, 1), :].broadcast_to([P, 2, D]),
                                             ALU.mult, ALU.add).then_inc(y_read, 1)
                if nxt:
                    do_rec_hi(st, -1)
                if yt:
                    dve.wait_ge(old_in[slot], st.val(off, 2, 32, 32))
                    dve.wait_ge(y_read, st.val(off, plus=1))
                    for h in range(2):
                        ins = dve.scalar_tensor_tensor(res[:, slot, h], res[:, slot, h],
                                                       wsel[:, st.slot(off, 4), h:h + 1], old[:, slot, h],
                                                       ALU.mult, ALU.add)
                    ins.then_inc(res_done, 1)
                if nxt:
                    do_rec_lo(st, -1)
                if st.at(-3, GRAPHS):
                    do_stats(st, -3)
                off = LAG
                if st.at(off, NF):
                    par = st.slot(off, 2)
                    for q in range(FC // 2):
                        if q == 2:
                            routing_between(st)
                        dve.wait_ge(h_hi, st.val(off, 1, FC // 2, q + 1))
                        cols = slice(q * 2 * SLOTS, (q + 1) * 2 * SLOTS)
                        dve.scalar_tensor_tensor(hidden[:, par, 1, cols], h32[:, q % 2, :], HS,
                                                 hidden[:, par, 0, cols], ALU.mult, ALU.subtract).then_inc(h_done, 1)
                else:
                    routing_between(st)
                off = LAG - 1
                if st.at(off, NF):
                    slot = st.slot(off, 2)
                    if st.slot(off, 4) == 0:
                        wait_alone(dve, list_done, min_list(st, off))
                    e = load_expert(dve, st, off)
                    dve.wait_ge(rows_in[slot], st.val(off, 2, 16, 16))
                    dve.tensor_copy(tok[:, st.slot(off, 4), :][:, :, None],
                                    rows[:, slot, :, COL_TOK:ROW].bitcast(I32))
                    dve.tensor_copy(wsel[:, st.slot(off, 4), :][:, :, None],
                                    rows[:, slot, :, COL_W:COL_TOK].bitcast(F32)[:, :, bass.DynSlice(e, 1)]
                                    ).then_inc(meta_done, 1)
                if st.at(0, GRAPHS):
                    dve.wait_ge(gnn_done, st.val(0, plus=1))
                    dve.tensor_reduce(amax[:, 0:1], ps_gnn, AX.X, ALU.max)
                    dve.tensor_reduce(lg[:, st.slot(0, GROUP), :], ps_lg.rearrange("p (k e) -> p e k", k=2), AX.X,
                                      ALU.add).then_inc(amax_done, 1)
                    dve.wait_ge(amax_done, st.val(0, plus=1))
                    dve.tensor_scalar(amax[:, 1:2], amax[:, 0:1], 1 / (XS * WS), gb_col[:, 0:1],
                                      ALU.mult, ALU.add).then_inc(amax_mid, 1)
                    dve.wait_ge(amax_mid, st.val(0, 1, 2, 1))
                    dve.tensor_scalar(amax[:, 2:3], amax[:, 1:2], 0.0, None, ALU.max).then_inc(amax_mid, 1)
                    dve.wait_ge(amax_mid, st.val(0, 1, 2, 2))
                    slot = st.slot(0, 8)
                    dve.tensor_scalar(xin[:, slot, :], xin[:, slot, :], amax[:, 2:3], None,
                                      ALU.add).then_inc(init_done, 1)
                routing(st)

            steps(dve, body)

        @block.tensor
        def _(pe):
            pe.wait_ge(const_in, 16 * 6)
            pe.wait_ge(pool_set, 2)
            pe.transpose(ps1[0][:, 0:P], adj_in[:], identf[:])
            pe.transpose(ps1[1][:, 0:E * FC], h32[0:E * FC, 0, 0:P], identf[0:E * FC, 0:E * FC]).then_inc(pe_set, 1)
            pe.wait_ge(dve_set, 2)

            def products(psum, parts):
                for n, (a, b) in enumerate(parts):
                    ins = pe.matmul(psum, a, b, start=n == 0, stop=n == len(parts) - 1)
                return ins

            def routing(st):
                part = st.i % GROUP
                if part == 0 and st.at(GROUP, GRAPHS):
                    pe.wait_ge(chosen_done, st.val(GROUP, GROUP, 1, 1))
                    if st.later(GROUP, GROUP):
                        pe.wait_ge(pos_read, st.val(GROUP, GROUP))
                    pe.matmul(ps_pos, before[:], chosen[:], start=True, stop=False)
                    for k in range(GROUP):
                        ins = pe.matmul(ps_pos[:, k + 1:, :], ones[:],
                                        chosen[:, k:k + 1, :].broadcast_to([P, GROUP - k, E]),
                                        start=False, stop=k == GROUP - 1)
                    ins.then_inc(pos_done, 1)
                if part == 1 and st.at(GROUP + 1, GRAPHS):
                    wait_alone(pe, new_tiles, st.val(GROUP + 1, GROUP, 1, 1))
                    first_entries()
                if part == 3 and st.at(GROUP + 3, GRAPHS):
                    wait_alone(pe, entries_done, st.val(GROUP + 3, GROUP, 1, 1))
                    if st.later(GROUP + 3, 3 * GROUP):
                        wait_alone(pe, list_done, st.val(GROUP + 3, GROUP, 1, -2))
                    whole_list()
                if st.reg is None and st.first == GRAPHS + GROUP + 1:
                    pe.wait_ge(new_tiles, NG + 1)
                    first_entries()
                if st.reg is None and st.first == GRAPHS + GROUP + 2:
                    pe.wait_ge(entries_done, NG + 1)
                    pe.wait_ge(list_done, NG - 2)
                    whole_list()

            def first_entries():
                pe.matmul(ps_first, beforef[:], ev[:, 2:3], start=True, stop=False)
                pe.matmul(ps_first, onesf[:], ev[:, 0:1], start=False, stop=True).then_inc(first_done, 1)

            def whole_list():
                pe.matmul(ps_list, ones[0:E, 0:1], entries[:], start=True, stop=True).then_inc(list_psum, 1)

            def body(st):
                if st.at(0, GRAPHS):
                    pe.wait_ge(rec_done, st.val(0, plus=1))
                    if st.later(0, 1):
                        pe.wait_ge(amax_done, st.val(0))
                    for c in range(4):
                        ins = pe.transpose(ps_xta[:, c * P:(c + 1) * P], rec[:, st.slot(0, 8), c * P:(c + 1) * P].bitcast(F16),
                                           ident[:])
                    ins.then_inc(xta_psum, 1)
                off = LAG
                if st.at(off, NF):
                    slot = st.slot(off, 2)
                    if st.slot(off, 4) == 0:
                        pe.wait_ge(list_done, min_list(st, off))
                    if st.reg is None and st.first == off:
                        pe.wait_ge(w_hi, 2 * E)
                        pe.wait_ge(w_lo, 2 * E)
                    e = load_expert(pe, st, off)
                    pe.wait_ge(xt_done, st.val(off, plus=1))
                    for c in range(FC):
                        if c % 2 == 0 and st.later(off, 1):
                            pe.wait_ge(gelu_done, st.val(off, 1, FC, c + 2 - FC))
                        parts = []
                        for dc in range(DC):
                            xh, xl = (xt[:, slot, k, dc * SLOTS:(dc + 1) * SLOTS] for k in range(2))
                            wh, wl = (w_cols[:, bass.DynSlice(e * (4 * DC * DFF) + (k * DC * DFF + dc * DFF + c * P), P)]
                                      for k in range(2))
                            parts += [(wh, xh), (wh, xl), (wl, xh)]
                        products(ps1[c // 2][:, c % 2 * SLOTS:(c % 2 + 1) * SLOTS], parts).then_inc(h_psum, 1)
                off = LAG - 1
                if st.at(off, NF):
                    slot = st.slot(off, 2)
                    pe.wait_ge(rows_in[slot], st.val(off, 2, 16, 16))
                    if st.later(off, 1):
                        pe.wait_ge(xt_done, st.val(off))
                    for h in range(2):
                        for c in range(4):
                            ins = pe.transpose(ps_xt[:, c // 2, (c % 2 * 2 + h) * P:(c % 2 * 2 + h + 1) * P],
                                               rows[:, slot, h, c * P:(c + 1) * P].bitcast(F16), ident[:])
                    ins.then_inc(xt_psum, 1)
                routing(st)

                if st.at(0, GRAPHS):
                    pe.wait_ge(xta_done, st.val(0, plus=1))
                    slot = st.slot(0, 8)
                    products(ps_lg,
                             [(xta[:, st.slot(0, 2), c * P:(c + 1) * P], wr16[:, c % 2, :]) for c in range(4)])
                    hi, lo = (rec[:, slot, k * D:(k + 1) * D].bitcast(F16) for k in range(2))
                    products(ps_gnn, [(adj_t[:, 0], hi), (adj_t[:, 0], lo), (adj_t[:, 1], hi)]).then_inc(gnn_done, 1)
                off = LAG + 1
                if st.at(off, NF):
                    slot = st.slot(off, 2)
                    e = load_expert(pe, st, off)
                    if st.later(off, 1):
                        pe.wait_ge(y_read, st.val(off))
                    for c in range(FC):
                        if c % 2 == 0:
                            pe.wait_ge(h_done, st.val(off, 1, FC // 2, c // 2 + 1))
                        wh, wl = (w_cols[:, bass.DynSlice(e * (4 * DC * DFF) + ((2 + k) * DC * DFF + c * D), D)]
                                  for k in range(2))
                        for n, (k, w) in enumerate(((0, wh), (1, wh), (0, wl))):
                            for h in range(2):
                                ins = pe.matmul(psy[:, h, :],
                                                hidden[:, slot, k, c * SLOTS + h * P:c * SLOTS + (h + 1) * P], w,
                                                start=c == 0 and n == 0 and h == 0, stop=c == FC - 1 and n == 2 and h == 1)
                    ins.then_inc(y_psum, 1)

            w_cols = w_all[:].rearrange("p e k c -> p (e k c)")
            steps(pe, body)


_INS = ["x", "adj", "L0_gnn_b", "L0_ffn_Wr", "L0_ffn_br", "L0_ffn_W1", "L0_ffn_b1", "L0_ffn_W2", "L0_ffn_b2"]


def kernel(**inputs):
    import concourse.bacc as bacc
    from concourse.bass_utils import run_bass_kernel_spmd

    nc = bacc.Bacc("TRN2", target_bir_lowering=False, num_devices=1)
    arrays, args = {}, []
    for name in _INS:
        a = np.ascontiguousarray(inputs[name])
        arrays[f"in_{name}"] = a
        args.append(nc.dram_tensor(f"in_{name}", a.shape, mybir.dt.from_np(a.dtype), kind="ExternalInput").ap())
    out = nc.dram_tensor("out", (GRAPHS, NODES, D), F32, kind="ExternalOutput").ap()
    build(nc, *args, out)
    result = run_bass_kernel_spmd(nc, [arrays], core_ids=[0])
    return result.results[0]["out"]
```

```python
from contextlib import ExitStack

import numpy as np

import concourse.bass as bass
from concourse import mybir

F32, F16, I32, U16 = mybir.dt.float32, mybir.dt.float16, mybir.dt.int32, mybir.dt.uint16
ALU = mybir.AluOpType
ACT = mybir.ActivationFunctionType
AX = mybir.AxisListType

P = 128
GRAPHS, NODES, D, DFF, E, K = 128, 128, 256, 1024, 8, 2
TOKENS = GRAPHS * NODES
EPS = 1e-5
CAP = int(np.ceil(1.25 * TOKENS * K / E))

GROUP = 4
NG = GRAPHS // GROUP
SLOTS = 2 * P
NF = TOKENS * K // SLOTS + E - 1
DC, FC = D // P, DFF // P
RTILES = TOKENS // SLOTS + 1
REGION = RTILES * SLOTS
EMPTY_TILE = E * RTILES
ROW = 2 * D + 2 * E + 2
COL_W, COL_TOK = 2 * D, 2 * D + 2 * E

ENTRY_BITS = 7
DEFAULT = (E - 1) * 128 + EMPTY_TILE - (E - 1) * RTILES

XS, WS, HS = 2.0**11, 2.0**8, 2.0**6
LAG = 18
STEPS = NF + LAG + 3
UNROLL = 8


class Step:

    def __init__(self, i, u, reg=None, turns=1):
        self.i, self.u, self.reg = i, u, reg
        self.first = UNROLL * u + i
        self.last = self.first + UNROLL * (turns - 1)

    def at(self, off, limit):
        a, b = (0 <= t - off < limit for t in (self.first, self.last))
        assert a == b
        return a

    def later(self, off, n):
        a, b = (t - off >= n for t in (self.first, self.last))
        assert a == b
        return a

    def val(self, off=0, div=1, mult=1, plus=0):
        base = mult * ((self.first - off) // div) + plus
        return base if self.reg is None else self.reg * (UNROLL // div * mult) + base

    def slot(self, off, n):
        return (self.i - off) % n


def steps(eng, body):
    def run(u0, u1):
        for u in range(u0, u1):
            for i in range(UNROLL):
                if UNROLL * u + i < STEPS:
                    body(Step(i, u))

    def loop(u0, u1):
        with eng.Fori(0, u1 - u0) as reg:
            for i in range(UNROLL):
                body(Step(i, u0, reg, u1 - u0))

    full = (LAG + 3) // UNROLL + 1
    drain = GRAPHS // UNROLL
    run(0, full)
    loop(full, drain - 1)
    run(drain - 1, STEPS // UNROLL + 1)


def build(nc, x, adj, gnn_b, Wr, br, W1, b1, W2, b2, out):
    x_rows = x.rearrange("b p c -> (b p) c")
    out_rows = out.rearrange("b p c -> (b p) c")
    out_words = out_rows.bitcast(I32)
    records = nc.dram_tensor("records", [(EMPTY_TILE + 1) * SLOTS, ROW], U16, kind="Internal").ap()

    with ExitStack() as ctx:
        def sb(name, shape, dt):
            return ctx.enter_context(nc.sbuf_tensor(name, shape, dt))

        def sem(name):
            return ctx.enter_context(nc.semaphore(name))

        w_all = sb("w_all", [P, E, 4, DC * DFF], F16)
        b1_col = sb("b1_col", [P, E * FC], F32)
        b2_bc = sb("b2_bc", [P, E, D], F32)
        hidden = sb("hidden", [P, 2, 2, FC * SLOTS], F16)
        stage = hidden[:].bitcast(F32).rearrange("p a b c -> p (a b) c")
        h32 = sb("h32", [P, 2, 2 * SLOTS], F32)
        rows = sb("rows", [P, 2, 2, ROW], U16)
        xt = sb("xt", [P, 2, 2, 2 * SLOTS], F16)
        tok = sb("tok", [P, 4, 2], I32)
        wsel = sb("wsel", [P, 4, 2], F32)
        old = sb("old", [P, 2, 2, D], F32)
        res = sb("res", [P, 2, 2, D], F32)
        xin = sb("xin", [P, 8, D], F32)
        xs = sb("xs", [P, 2, D], F32)
        rec = sb("rec", [P, 8, ROW], U16)
        xta = sb("xta", [P, 2, 4 * P], F16)
        stats = sb("stats", [P, 4, 6], F32)
        mv = sb("mv", [P, 4, 2], F32)
        var_eps = sb("var_eps", [P, 2], F32)
        minus_half = sb("minus_half", [P, 1], F32)
        rstd = sb("rstd", [P, 4], F32)
        amax = sb("amax", [P, 2], F32)
        ident = sb("ident", [P, P], F16)
        identf = sb("identf", [P, P], F32)
        before = sb("before", [P, P], F16)
        beforef = sb("beforef", [E, E], F32)
        ones = sb("ones", [P, P], F16)
        onesf = sb("onesf", [E, E], F32)
        iota_i = sb("iota_i", [P, 1 + NF], I32)
        rank = sb("rank", [P, E], F32)
        region_row = sb("region_row", [P, E], F32)
        entry_no = sb("entry_no", [E, NF], F32)
        entry_base = sb("entry_base", [E, 1], F32)
        part_no = sb("part_no", [P, 1], F32)
        tok_no = sb("tok_no", [P, GROUP], F32)
        pad_rec = sb("pad_rec", [P, ROW], U16)
        adj_in = sb("adj_in", [P, P], F32)
        adj_t = sb("adj_t", [P, 2, P], F16)
        wr_in = sb("wr_in", [P, DC, E], F32)
        wr16 = sb("wr16", [P, DC, 2 * E], F16)
        br_bc = sb("br_bc", [P, E], F32)
        gb_col = sb("gb_col", [P, 1], F32)
        lg = sb("lg", [P, GROUP, E], F32)
        r = {n: sb("r_" + n, [P, GROUP, E], F32) for n in (
            "L", "eq", "rk", "oh1", "L2", "oh2", "D", "E", "W", "pos", "keep", "v1", "v2")}
        s = {n: sb("s_" + n, [P, GROUP], F32) for n in (
            "m1", "r1", "m2", "r2", "sum", "inv", "row1", "row2")}
        chosen = sb("chosen", [P, GROUP + 1, E], F16)
        dest = sb("dest", [P, 2, K, GROUP], I32)
        count = sb("count", [P, E], F32)
        ev_cc = sb("ev_cc", [E, E], F32)
        ev_i = sb("ev_i", [E, 2], I32)
        ev = sb("ev", [E, 7], F32)
        ev_a = sb("ev_a", [E, NF], F32)
        ev_b = sb("ev_b", [E, NF], F32)
        entries = sb("entries", [E, NF], F16)
        entry_t = sb("entry_t", [1, NF], I32)
        expert_t = sb("expert_t", [1, NF], I32)
        rowtile_t = sb("rowtile_t", [1, NF], I32)
        count_t = sb("count_t", [1, E], I32)

        ps1 = [ctx.enter_context(nc.psum_tensor(f"ps1_{k}", [P, 2 * SLOTS], F32)) for k in range(4)]
        psy = ctx.enter_context(nc.psum_tensor("psy", [P, 2, D], F32))
        ps_xt = ctx.enter_context(nc.psum_tensor("ps_xt", [P, 2, 2 * SLOTS], F16))
        psa = ctx.enter_context(nc.psum_tensor("psa", [P, 512], F32))
        ps_xta = psa[:, 0:2 * P].bitcast(F16)
        ps_lg = psa[:, 0:2 * E]
        ps_gnn = psa[:, 2 * P:2 * P + D]
        pss = ctx.enter_context(nc.psum_tensor("pss", [P, 512], F32))
        ps_pos = pss[:, 128:128 + (GROUP + 1) * E].rearrange("p (t e) -> p t e", e=E)
        ps_first = pss[0:E, 176:177]
        ps_list = pss[0:1, 192:192 + NF]

        const_in = sem("const_in")
        x_in = [sem(f"x_in{k}") for k in range(4)]
        w_in = [sem(f"w_in{k}") for k in range(4)]
        rows_in = [sem(f"rows_in{k}") for k in range(2)]
        old_in = [sem(f"old_in{k}") for k in range(2)]
        init_out = [sem(f"init_out{k}") for k in range(4)]
        scattered = [sem(f"scattered{k}") for k in range(8)]
        added = [sem(f"added{k}") for k in range(2)]
        empty_out = sem("empty_out")
        pads_out = sem("pads_out")
        pool_set = sem("pool_set")
        dve_set = sem("dve_set")
        pe_set = sem("pe_set")
        act_set = sem("act_set")
        w_scaled = sem("w_scaled")
        w_hi = sem("w_hi")
        w_lo_pool = sem("w_lo_pool")
        w_lo_dve = sem("w_lo_dve")
        stats_done = sem("stats_done")
        stats_mid = sem("stats_mid")
        var_done = sem("var_done")
        rstd_done = sem("rstd_done")
        xs_done = sem("xs_done")
        rec_hi = sem("rec_hi")
        rec_done = sem("rec_done")
        xta_psum = sem("xta_psum")
        xta_done = sem("xta_done")
        gnn_done = sem("gnn_done")
        amax_done = sem("amax_done")
        amax_mid = sem("amax_mid")
        init_done = sem("init_done")
        diff_done = sem("diff_done")
        chosen_done = sem("chosen_done")
        exp_done = sem("exp_done")
        pos_done = sem("pos_done")
        pos_read = sem("pos_read")
        routed = sem("routed")
        new_tiles = sem("new_tiles")
        first_done = sem("first_done")
        entries_done = sem("entries_done")
        list_psum = sem("list_psum")
        list_done = sem("list_done")
        counts_done = sem("counts_done")
        norm_done = sem("norm_done")
        chain = sem("chain")
        table_links = sem("table_links")
        meta_done = sem("meta_done")
        xt_psum = sem("xt_psum")
        xt_done = sem("xt_done")
        h_psum = sem("h_psum")
        gelu_done = sem("gelu_done")
        h_hi = sem("h_hi")
        h_done = sem("h_done")
        y_psum = sem("y_psum")
        y_read = sem("y_read")
        res_done = sem("res_done")

        waits_alone = {eng.engine: sem(f"waits_alone_{n}") for n, eng in (
            ("pool", nc.gpsimd), ("dve", nc.vector), ("pe", nc.tensor))}

        block = ctx.enter_context(nc.Block())

        def table(t, st, off, n=1):
            return t[0:1, bass.DynSlice(st.val(off), n)] if st.reg is not None else t[0:1, st.val(off):st.val(off) + n]

        def w_half(k, part):
            half = DC * DFF // 2
            return w_all[:, k // 4, 2 * (k // 2 % 2) + part, k % 2 * half:(k % 2 + 1) * half]

        lo_by_pool = [k for k in range(4 * E) if k % 2 == 0 or k // 2 % GROUP < 2]

        def wait_lo(eng, k):
            by_pool = sum(i <= k for i in lo_by_pool)
            if k in lo_by_pool:
                eng.wait_ge(w_lo_pool, by_pool)
            else:
                eng.wait_ge(w_lo_dve, k + 1 - by_pool)

        def load_expert(eng, st, off):
            return eng.value_load(table(expert_t, st, off), min_val=0, max_val=E - 1)

        def wait_alone(eng, semaphore, value):
            eng.wait_ge(semaphore, value)
            eng.sem_inc(waits_alone[eng.engine], 1)

        def min_list(st, off):
            return NG - 1 if st.later(off, GROUP * (NG - 2)) else st.val(off, GROUP, 1, 1)

        @block.sync
        def _(sp):
            def x_load(st, off):
                pair = st.slot(off, 8) // 2
                src = x_rows.rearrange("(t p) c -> p t c", p=P)
                t0 = st.val(off)
                tiles = src[:, bass.DynSlice(t0, 2), :] if st.reg is not None else src[:, t0:t0 + 2, :]
                sp.dma_start(xin[:, 2 * pair:2 * pair + 2, :], tiles).then_inc(x_in[pair], 16)

            def w_load(k):
                if k >= 4:
                    sp.wait_ge(w_hi, k - 3)
                    wait_lo(sp, k - 4)
                m = k // 2
                c = (DC, FC)[m % 2] // 2
                src = (W1, W2)[m % 2][m // 2].rearrange("(c p) f -> p c f", p=P)[:, k % 2 * c:(k % 2 + 1) * c, :]
                sp.dma_start(stage[:, k % 4, :].rearrange("p (c f) -> p c f", c=c), src).then_inc(w_in[k % 4], 16)

            x_load(Step(0, 0), 0)
            x_load(Step(2, 0), 0)
            sp.dma_start(adj_in[:], adj).then_inc(const_in, 16)
            sp.dma_start(wr_in[:], Wr.rearrange("(c p) e -> p c e", p=P)).then_inc(const_in, 16)
            sp.dma_start(br_bc[:], br.rearrange("(a e) -> a e", a=1).broadcast_to([P, E])).then_inc(const_in, 16)
            sp.dma_start(gb_col[:], gnn_b.rearrange("(p a) -> p a", a=1)).then_inc(const_in, 16)
            sp.dma_start(h32[0:E * FC, 0, 0:P], b1.rearrange("e (c p) -> (e c) p", p=P)).then_inc(const_in, 16)
            sp.dma_start(b2_bc[:], b2.rearrange("(a e) d -> a e d", a=1).broadcast_to([P, E, D])).then_inc(const_in, 16)
            sp.wait_ge(pool_set, 4)
            for h in range(2):
                r0 = EMPTY_TILE * SLOTS + h * P
                sp.dma_start(records[r0:r0 + P, :], pad_rec[:]).then_inc(empty_out, 16)

            def body(st):
                if st.reg is None and st.first < 2 * E:
                    w_load(2 * st.first)
                    w_load(2 * st.first + 1)
                off = LAG - 2
                if st.at(off, NF):
                    if st.slot(off, 4) == 0:
                        m = (st.first - off) // GROUP
                        if st.later(off, GROUP * (NG - 2)):
                            if st.first - off == GROUP * (NG - 2):
                                sp.wait_ge(list_done, NG - 1)
                                sp.wait_ge(pads_out, 16 * 2 * E)
                                sp.wait_ge(empty_out, 32)
                        else:
                            sp.wait_ge(list_done, st.val(off, GROUP, 1, 1))
                            for k in range(GROUP):
                                sp.wait_ge(scattered[st.slot(off - 2 * GROUP, 8) + k],
                                           st.val(off - 2 * GROUP, 8, 32, 32))
                    if st.later(off, 2):
                        sp.wait_ge(xt_psum, st.val(off, plus=-1))
                        sp.wait_ge(meta_done, st.val(off, plus=-1))
                    q = sp.value_load(table(rowtile_t, st, off), min_val=0, max_val=EMPTY_TILE)
                    src = records.rearrange("(n h p) c -> n p h c", h=2, p=P)[bass.DynSlice(q, 1)]
                    slot = st.slot(off, 2)
                    sp.dma_start(rows[:, slot], src.rearrange("n p h c -> p (n h) c")).then_inc(rows_in[slot], 16)
                if st.i % 2 == 0 and st.at(-4, GRAPHS):
                    if st.later(4, 0):
                        for k in range(2):
                            sp.wait_ge(init_out[st.slot(4, 4) + k], st.val(4, 4, 16, 16))
                    x_load(st, -4)
                if st.at(1, GRAPHS):
                    sp.wait_ge(init_done, st.val(0))
                    src = xin[:, st.slot(1, 8), :]
                    dst = out_rows.rearrange("(t p) c -> t p c", p=P)
                    t0 = st.val(1)
                    dst = dst[bass.DynSlice(t0, 1)].rearrange("t p c -> (t p) c") if st.reg is not None else dst[t0]
                    sp.dma_start(dst, src).then_inc(init_out[st.slot(1, 4)], 16)
                if st.reg is None and st.first == GRAPHS + 2:
                    sp.wait_ge(counts_done, 1)
                    for e in range(E):
                        n = sp.value_load(count_t[0:1, e:e + 1], min_val=0, max_val=TOKENS)
                        for h in range(2):
                            dst = records[bass.DynSlice(n + (e * REGION + h * P), P), :]
                            sp.dma_start(dst, pad_rec[:]).then_inc(pads_out, 16)

            steps(sp, body)
            for k in range(2):
                sp.wait_ge(added[k], 32 * ((NF + 1 - k) // 2))

        @block.gpsimd
        def _(pool):
            pool.memset(ident[:], 0.0)
            pool.memset(identf[:], 0.0)
            pool.memset(before[:], 1.0)
            pool.memset(pad_rec[:], 0)
            pool.memset(minus_half[:], -0.5)
            pool.memset(beforef[:], 1.0)
            pool.memset(onesf[:], 1.0)
            pool.memset(ones[:], 1.0)
            pool.memset(old[:], 0.0).then_inc(pool_set, 1)
            pool.wait_ge(pool_set, 1)
            pool.affine_select(out=ident[:], in_=ident[:], compare_op=ALU.not_equal, fill=1.0, base=0,
                               pattern=[[-1, P]], channel_multiplier=1)
            pool.affine_select(out=identf[:], in_=identf[:], compare_op=ALU.not_equal, fill=1.0, base=0,
                               pattern=[[-1, P]], channel_multiplier=1)
            pool.affine_select(out=before[:], in_=before[:], compare_op=ALU.is_gt, fill=0.0, base=0,
                               pattern=[[1, P]], channel_multiplier=-1)
            pool.affine_select(out=beforef[:], in_=beforef[:], compare_op=ALU.is_gt, fill=0.0, base=0,
                               pattern=[[1, E]], channel_multiplier=-1).then_inc(pool_set, 1)
            pool.iota(iota_i[:, 0:1], pattern=[[0, 1]], base=0, channel_multiplier=1)
            pool.iota(iota_i[:, 1:1 + NF], pattern=[[1, NF]], base=0, channel_multiplier=0).then_inc(pool_set, 1)
            pool.memset(pad_rec[:, COL_TOK:ROW].bitcast(I32), TOKENS).then_inc(pool_set, 1)

            def inverse_deviation(st, off):
                slot = st.slot(off, 4)
                wait_alone(pool, stats_done, st.val(off, plus=1))
                two = st.slot(off, 2)
                pool.tensor_scalar(var_eps[:, two:two + 1], mv[:, slot, 1:2], EPS, None, ALU.add).then_inc(var_done, 1)
                pool.wait_ge(var_done, st.val(off, plus=1))
                pool.tensor_tensor(rstd[:, slot:slot + 1], var_eps[:, two:two + 1], minus_half[:],
                                   ALU.pow).then_inc(rstd_done, 1)

            def records_out(st, off, par):
                slot = st.slot(off, 8)
                for k in range(K):
                    pool.indirect_dma_start(
                        out=records, out_offset=bass.IndirectOffsetOnAxis(
                            ap=dest[:, par, k, slot % GROUP:slot % GROUP + 1], axis=0),
                        in_=rec[:, slot, :], in_offset=None).then_inc(scattered[slot], 16)

            def body(st):
                off = LAG + 2
                if st.at(off, NF):
                    slot = st.slot(off, 2)
                    wait_alone(pool, res_done, st.val(off, plus=1))
                    for h in range(2):
                        pool.indirect_dma_start(
                            out=out_rows, out_offset=bass.IndirectOffsetOnAxis(
                                ap=tok[:, st.slot(off, 4), h:h + 1], axis=0),
                            in_=res[:, slot, h, :], in_offset=None,
                            bounds_check=TOKENS - 1, oob_is_err=False).then_inc(added[slot], 16)
                if st.i % GROUP >= 2:
                    first = st.i % GROUP * 2 - 4
                    goff = GROUP + st.i % 4 - first
                    if st.at(goff, GRAPHS):
                        if first == 0:
                            wait_alone(pool, routed, st.val(goff, GROUP, 1, 1))
                        records_out(st, goff, st.slot(goff, 8) // GROUP)
                        records_out(st, goff - 1, st.slot(goff, 8) // GROUP)
                off = LAG + 1
                if st.at(off, NF):
                    slot = st.slot(off, 2)
                    wait_alone(pool, meta_done, st.val(off, plus=1))
                    if st.later(off, 1):
                        wait_alone(pool, added[1 - slot], st.val(off + 1, 2, 32, 32))
                    if st.slot(off, 4) == 0 and not st.later(off, GROUP * (NG - 2)):
                        for k in range(4):
                            wait_alone(pool, init_out[k], st.val(off - 2 * GROUP, GROUP, 16, 16))
                    for h in range(2):
                        pool.indirect_dma_start(
                            out=old[:, slot, h, :].bitcast(I32), out_offset=None, in_=out_words,
                            in_offset=bass.IndirectOffsetOnAxis(ap=tok[:, st.slot(off, 4), h:h + 1], axis=0),
                            bounds_check=TOKENS - 1, oob_is_err=False).then_inc(old_in[slot], 16)
                if st.at(-3, GRAPHS):
                    inverse_deviation(st, -3)
                if st.reg is None and st.first < 2 * E:
                    for k in (2 * st.first, 2 * st.first + 1):
                        if k in lo_by_pool:
                            pool.wait_ge(w_hi, k + 1)
                            pool.tensor_tensor(w_half(k, 1), stage[:, k % 4, :], w_half(k, 0),
                                               ALU.subtract).then_inc(w_lo_pool, 1)

            for t in range(3):
                inverse_deviation(Step(t, 0), 0)
            steps(pool, body)

        @block.scalar
        def _(act):
            act.wait_ge(pe_set, 1)
            act.activation(adj_t[:, 0, :], ps1[0][:, 0:P], ACT.Copy, scale=WS)
            act.activation(b1_col[:], ps1[1][:, 0:E * FC], ACT.Copy).then_inc(act_set, 1)

            def body(st):
                if st.at(0, GRAPHS):
                    act.wait_ge(xta_psum, st.val(0, plus=1))
                    if st.later(0, 2):
                        act.wait_ge(gnn_done, st.val(0, plus=-1))
                    act.activation(xta[:, st.slot(0, 2), :], ps_xta, ACT.Copy).then_inc(xta_done, 1)
                if st.i % GROUP == 0 and st.at(GROUP, GRAPHS):
                    act.wait_ge(diff_done, st.val(GROUP, GROUP, 1, 1))
                    if st.later(GROUP, GROUP):
                        act.wait_ge(routed, st.val(GROUP, GROUP))
                    act.activation(r["E"][:], r["D"][:], ACT.Exp).then_inc(exp_done, 1)
                if st.reg is None and st.first < 2 * E:
                    for k in (2 * st.first, 2 * st.first + 1):
                        act.wait_ge(w_in[k % 4], 16 * (k // 4 + 1))
                        act.activation(stage[:, k % 4, :], stage[:, k % 4, :], ACT.Copy, scale=WS).then_inc(w_scaled, 1)
                        act.wait_ge(w_scaled, k + 1)
                        act.activation(w_half(k, 0), stage[:, k % 4, :], ACT.Copy).then_inc(w_hi, 1)
                off = LAG
                if st.at(off, NF):
                    e = load_expert(act, st, off)
                    par = st.slot(off, 2)

                    def gelu(q):
                        act.wait_ge(h_psum, st.val(off, 1, FC, 2 * q + 2))
                        if st.later(off, 1) or q >= 2:
                            act.wait_ge(h_done, st.val(off, 1, FC // 2, q - 1))
                        for c in (2 * q, 2 * q + 1):
                            act.activation(h32[:, q % 2, c % 2 * SLOTS:(c % 2 + 1) * SLOTS],
                                           ps1[q][:, c % 2 * SLOTS:(c % 2 + 1) * SLOTS], ACT.Gelu,
                                           bias=b1_col[:, bass.DynSlice(e * FC + c, 1)],
                                           scale=1 / (XS * WS)).then_inc(gelu_done, 1)

                    def hi(q):
                        act.wait_ge(gelu_done, st.val(off, 1, FC, 2 * q + 2))
                        if q == 0 and st.later(off, 2):
                            act.wait_ge(y_psum, st.val(off, plus=-1))
                        if q == 0 and not st.later(off, 2):
                            act.wait_ge(w_hi, 4 * E)
                            act.wait_ge(w_lo_pool, len(lo_by_pool))
                            act.wait_ge(w_lo_dve, 4 * E - len(lo_by_pool))
                        act.activation(hidden[:, par, 0, q * 2 * SLOTS:(q + 1) * 2 * SLOTS], h32[:, q % 2, :],
                                       ACT.Copy, scale=HS).then_inc(h_hi, 1)

                    gelu(0)
                    gelu(1)
                    hi(0)
                    hi(1)
                    gelu(2)
                    gelu(3)
                    hi(2)
                    hi(3)
                off = LAG - 1
                if st.at(off, NF):
                    act.wait_ge(xt_psum, st.val(off, plus=1))
                    if st.later(off, 2):
                        act.wait_ge(h_psum, st.val(off, 1, FC, -FC))
                    act.activation(xt[:, st.slot(off, 2)], ps_xt[:], ACT.Copy).then_inc(xt_done, 1)

            steps(act, body)

        @block.vector
        def _(dve):
            links = [0]

            def link(ins):
                links[0] += 1
                ins.then_inc(dve_set, 1)
                dve.wait_ge(dve_set, links[0])

            def do_stats(st, off):
                dve.wait_ge(x_in[st.slot(off, 8) // 2], st.val(off, 8, 16, 16))
                dve.bn_stats(stats[:, st.slot(off, 4), :], xin[:, st.slot(off, 8), :]).then_inc(stats_mid, 1)

            def do_aggr(st, off):
                wait_alone(dve, stats_mid, st.val(off, plus=1))
                dve.bn_aggr(mv[:, st.slot(off, 4), :], stats[:, st.slot(off, 4), :]).then_inc(stats_done, 1)

            def do_xs(st, off):
                slot = st.slot(off, 4)
                dve.wait_ge(rstd_done, st.val(off, plus=1))
                dve.tensor_scalar(xs[:, st.slot(off, 2), :], xin[:, st.slot(off, 8), :], mv[:, slot, 0:1],
                                  rstd[:, slot:slot + 1], ALU.subtract, ALU.mult).then_inc(xs_done, 1)

            def do_rec_hi(st, off):
                slot = st.slot(off, 8)
                if st.later(off, 8):
                    dve.wait_ge(scattered[slot], st.val(off, 8, 32))
                dve.wait_ge(xs_done, st.val(off, plus=1))
                dve.tensor_scalar(rec[:, slot, 0:D].bitcast(F16), xs[:, st.slot(off, 2), :], XS, None,
                                  ALU.mult).then_inc(rec_hi, 1)

            def do_rec_lo(st, off):
                slot = st.slot(off, 8)
                dve.wait_ge(rec_hi, st.val(off, plus=1))
                dve.scalar_tensor_tensor(rec[:, slot, D:2 * D].bitcast(F16), xs[:, st.slot(off, 2), :], XS,
                                         rec[:, slot, 0:D].bitcast(F16), ALU.mult, ALU.subtract).then_inc(rec_done, 1)

            for t in range(3):
                do_stats(Step(t, 0), 0)
                do_aggr(Step(t, 0), 0)
            dve.wait_ge(pool_set, 4)
            dve.memset(count[:], 0.0)
            dve.memset(chosen[:], 0.0)
            dve.memset(entries[:], 0.0)
            dve.memset(ev[:], 0.0)
            dve.tensor_scalar(rank[:], iota_i[:, 1:1 + E], -1.0, float(E), ALU.mult, ALU.add)
            dve.tensor_scalar(region_row[:], iota_i[:, 1:1 + E], float(REGION), None, ALU.mult)
            dve.tensor_copy(entry_no[:], iota_i[0:E, 1:1 + NF])
            dve.tensor_scalar(entry_base[:], iota_i[0:E, 0:1], 128.0, -float(DEFAULT), ALU.mult, ALU.add)
            dve.tensor_scalar(tok_no[:], iota_i[:, 1:1 + GROUP], float(P), None, ALU.mult)
            dve.wait_ge(const_in, 16 * 6)
            link(dve.tensor_scalar(wr16[:, :, 0:E], wr_in[:], WS, None, ALU.mult))
            dve.scalar_tensor_tensor(wr16[:, :, E:2 * E], wr_in[:], WS, wr16[:, :, 0:E], ALU.mult, ALU.subtract)
            dve.tensor_scalar(gb_col[:], gb_col[:], XS * WS, None, ALU.mult)
            dve.tensor_copy(part_no[:], iota_i[:, 0:1])
            dve.wait_ge(act_set, 1)
            link(dve.scalar_tensor_tensor(adj_t[:, 1, :], ps1[0][:, 0:P], WS, adj_t[:, 0, :], ALU.mult, ALU.subtract))
            link(dve.tensor_scalar(tok_no[:], tok_no[:], part_no[:, 0:1], None, ALU.add))
            do_xs(Step(0, 0), 0)
            do_rec_hi(Step(0, 0), 0)
            do_rec_lo(Step(0, 0), 0)

            TOP, SOFT, PLACE, FULL, REST, NEW = 12, 7, 1, 4, 7, 4
            PER_GROUP = TOP + SOFT + PLACE + FULL + REST + NEW

            class Chain:

                def __init__(self, st, off, start):
                    self.st, self.off, self.start, self.k = st, off, start, 0

                def __call__(self, ins):
                    self.k += 1
                    ins.then_inc(chain, 1)
                    dve.wait_ge(chain, self.st.val(self.off, GROUP, PER_GROUP, self.start + self.k))

            class TableLinks:

                def __init__(self, st):
                    self.st, self.k = st, 0

                def __call__(self, ins):
                    self.k += 1
                    ins.then_inc(table_links, 1)
                    dve.wait_ge(table_links, self.st.val(3 * GROUP + 3, GROUP, 2, self.k))

            def bc(a):
                return a[:, :, None].broadcast_to([P, GROUP, E])

            def over_tiles(a):
                return a[:, None, :].broadcast_to([P, GROUP, E])

            def top(link, values, m, rk, onehot):
                link(dve.tensor_reduce(s[m][:], values[:], AX.X, ALU.max))
                link(dve.tensor_tensor(r["eq"][:], values[:], bc(s[m]), ALU.is_equal))
                link(dve.tensor_tensor(r["rk"][:], r["eq"][:], over_tiles(rank), ALU.mult))
                link(dve.tensor_reduce(s[rk][:], r["rk"][:], AX.X, ALU.max))
                link(dve.tensor_tensor(onehot[:], r["rk"][:], bc(s[rk]), ALU.is_equal))

            def route_top(st, off):
                link = Chain(st, off, 0)
                dve.wait_ge(amax_done, st.val(off, GROUP, GROUP, GROUP))
                link(dve.scalar_tensor_tensor(r["L"][:], lg[:], 1 / (XS * WS), over_tiles(br_bc), ALU.mult, ALU.add))
                top(link, r["L"], "m1", "r1", r["oh1"])
                dve.tensor_tensor(r["D"][:], r["L"][:], bc(s["m1"]), ALU.subtract).then_inc(diff_done, 1)
                link(dve.scalar_tensor_tensor(r["L2"][:], r["oh1"][:], -1e30, r["L"][:], ALU.mult, ALU.add))
                top(link, r["L2"], "m2", "r2", r["oh2"])
                if st.later(off, GROUP):
                    dve.wait_ge(pos_done, st.val(off, GROUP))
                dve.tensor_tensor(chosen[:, 0:GROUP, :], r["oh1"][:], r["oh2"][:], ALU.add).then_inc(chosen_done, 1)
                dve.wait_ge(chosen_done, st.val(off, GROUP, 1, 1))
                assert link.k == TOP

            def softmax(st, off):
                link = Chain(st, off, TOP)
                dve.wait_ge(exp_done, st.val(off, GROUP, 1, 1))
                dve.tensor_tensor(r["W"][:], r["E"][:], chosen[:, 0:GROUP, :], ALU.mult)
                link(dve.tensor_reduce(s["sum"][:], r["E"][:], AX.X, ALU.add))
                link(dve.reciprocal(s["inv"][:], s["sum"][:]))
                link(dve.tensor_tensor(r["W"][:], r["W"][:], bc(s["inv"]), ALU.mult))
                link(dve.tensor_reduce(s["sum"][:], r["W"][:], AX.X, ALU.add))
                link(dve.tensor_scalar(s["sum"][:], s["sum"][:], 1e-9, None, ALU.add))
                link(dve.reciprocal(s["inv"][:], s["sum"][:]))
                link(dve.tensor_tensor(r["W"][:], r["W"][:], bc(s["inv"]), ALU.mult))
                assert link.k == SOFT

            def places(st, off):
                link = Chain(st, off, TOP + SOFT)
                dve.wait_ge(pos_done, st.val(off, GROUP, 1, 1))
                link(dve.tensor_tensor(r["pos"][:], ps_pos[:, 0:GROUP, :], over_tiles(count), ALU.add))
                dve.tensor_tensor(count[:], count[:], ps_pos[:, GROUP, :], ALU.add).then_inc(pos_read, 1)
                dve.wait_ge(pos_read, st.val(off, GROUP, 1, 1))

            def route_rest(st, off):
                link = Chain(st, off, TOP + SOFT + PLACE + FULL)
                par = st.slot(off, 8) // GROUP
                recs = rec[:, GROUP * par:GROUP * par + GROUP, :]
                link(dve.tensor_scalar(r["keep"][:], r["pos"][:], float(CAP), None, ALU.is_lt))
                link(dve.tensor_tensor(r["W"][:], r["W"][:], r["keep"][:], ALU.mult))
                link(dve.tensor_reduce(s["sum"][:], r["W"][:], AX.X, ALU.add))
                dve.tensor_scalar(s["sum"][:], s["sum"][:], 1e-9, None, ALU.add).then_inc(norm_done, 1)
                link(dve.tensor_tensor(r["pos"][:], r["pos"][:], over_tiles(region_row), ALU.add))
                dve.wait_ge(norm_done, st.val(off, GROUP, 1, 1))
                link(dve.reciprocal(s["inv"][:], s["sum"][:]))
                dve.tensor_tensor(recs[:, :, COL_W:COL_TOK].bitcast(F32), r["W"][:], bc(s["inv"]), ALU.mult)
                dve.tensor_copy(recs[:, :, COL_TOK:ROW].bitcast(I32), tok_no[:][:, :, None])
                dve.tensor_tensor(r["v1"][:], r["oh1"][:], r["pos"][:], ALU.mult)
                link(dve.tensor_tensor(r["v2"][:], r["oh2"][:], r["pos"][:], ALU.mult))
                dve.tensor_scalar(tok_no[:], tok_no[:], float(GROUP * P), None, ALU.add)
                dve.tensor_reduce(s["row1"][:], r["v1"][:], AX.X, ALU.add)
                link(dve.tensor_reduce(s["row2"][:], r["v2"][:], AX.X, ALU.add))
                dve.tensor_copy(dest[:, par, 0, :], s["row1"][:])
                dve.tensor_copy(dest[:, par, 1, :], s["row2"][:]).then_inc(routed, 1)
                dve.wait_ge(routed, st.val(off, GROUP, 1, 1))
                assert link.k == REST

            def full_tiles(link, up):
                link(dve.tensor_tensor(ev_cc[:], count[0:E, :], identf[0:E, 0:E], ALU.mult))
                link(dve.tensor_reduce(ev[:, 6:7], ev_cc[:], AX.X, ALU.add))
                link(dve.tensor_scalar(ev_i[:, 0:1], ev[:, 6:7], float(up), None, ALU.add))
                link(dve.tensor_scalar(ev_i[:, 1:2], ev_i[:, 0:1], int(np.log2(SLOTS)), None, ALU.logical_shift_right))
                dve.tensor_copy(ev[:, 1:2], ev_i[:, 1:2])
                dve.tensor_tensor(ev[:, 2:3], ev_i[:, 1:2], ev[:, 0:1], ALU.subtract).then_inc(new_tiles, 1)

            def list_new(link):
                dve.tensor_copy(ev[:, 3:4], ps_first)
                dve.tensor_tensor(ev[:, 4:5], ps_first, ev[:, 2:3], ALU.add)
                link(dve.scalar_tensor_tensor(ev[:, 5:6], ev[:, 0:1], entry_base[:, 0:1], ps_first,
                                              ALU.add, ALU.subtract))
                dve.tensor_copy(ev[:, 0:1], ev[:, 1:2])
                link(dve.tensor_scalar(ev_a[:], entry_no[:], ev[:, 3:4], None, ALU.is_ge))
                link(dve.scalar_tensor_tensor(ev_b[:], entry_no[:], ev[:, 4:5], ev_a[:], ALU.is_lt, ALU.mult))
                link(dve.scalar_tensor_tensor(ev_a[:], entry_no[:], ev[:, 5:6], ev_b[:], ALU.add, ALU.mult))
                dve.tensor_tensor(entries[:], entries[:], ev_a[:], ALU.add).then_inc(entries_done, 1)

            def tables(link, window, n):
                def win(t):
                    return t[0:1, window]
                link(dve.tensor_scalar(win(entry_t), ps_list[:, window], float(DEFAULT), None, ALU.add))
                link(dve.tensor_scalar(win(expert_t), win(entry_t), ENTRY_BITS, None, ALU.logical_shift_right))
                dve.scalar_tensor_tensor(win(rowtile_t), win(expert_t), float(RTILES - 128), win(entry_t),
                                         ALU.mult, ALU.add).then_inc(list_done, 1)

            def routing_between(st):
                part = st.i % GROUP
                if part == 0 and st.at(GROUP, GRAPHS):
                    softmax(st, GROUP)
                if part == 1 and st.at(GROUP + 1, GRAPHS):
                    route_rest(st, GROUP + 1)
                if part == 2 and st.at(GROUP + 2, GRAPHS):
                    dve.wait_ge(first_done, st.val(GROUP + 2, GROUP, 1, 1))
                    if st.later(GROUP + 2, GROUP):
                        dve.wait_ge(list_psum, st.val(GROUP + 2, GROUP))
                    list_new(Chain(st, GROUP + 2, TOP + SOFT + PLACE + FULL + REST))
                if part == 3 and st.at(GROUP + 3, GRAPHS) and st.later(GROUP + 3, 2 * GROUP):
                    dve.wait_ge(list_psum, st.val(GROUP + 3, GROUP, 1, 1))
                    first = st.val(3 * GROUP + 3, GROUP, GROUP)
                    tables(TableLinks(st), bass.DynSlice(first, GROUP) if st.reg is not None
                           else slice(first, first + GROUP), GROUP)

            def routing(st):
                part = st.i % GROUP
                if part == 3 and st.at(3, GRAPHS):
                    route_top(st, 3)
                if part == 0 and st.at(GROUP, GRAPHS):
                    places(st, GROUP)
                    if st.later(GROUP, GROUP):
                        dve.wait_ge(entries_done, st.val(GROUP, GROUP))
                    full_tiles(Chain(st, GROUP, TOP + SOFT + PLACE), 0)
                if st.reg is None:
                    if st.first == GRAPHS + 1:
                        dve.tensor_copy(count_t[:], count[0:1, :]).then_inc(counts_done, 1)
                    if st.first == GRAPHS + GROUP:
                        dve.wait_ge(entries_done, NG)
                        full_tiles(link, SLOTS - 1)
                    if st.first == GRAPHS + GROUP + 1:
                        dve.wait_ge(first_done, NG + 1)
                        dve.wait_ge(list_psum, NG)
                        list_new(link)
                    if st.first == GRAPHS + GROUP + 2:
                        dve.wait_ge(list_psum, NG + 1)
                        tables(link, slice(GROUP * (NG - 2), NF), NF - GROUP * (NG - 2))

            def body(st):
                nxt = st.at(-1, GRAPHS)
                if nxt:
                    do_xs(st, -1)
                if st.at(-3, GRAPHS):
                    do_stats(st, -3)
                off = LAG + 2
                yt = st.at(off, NF)
                if yt:
                    slot = st.slot(off, 2)
                    e = load_expert(dve, st, off)
                    if st.later(off, 2):
                        dve.wait_ge(added[slot], st.val(off, 2, 32))
                    dve.wait_ge(y_psum, st.val(off, plus=1))
                    dve.scalar_tensor_tensor(res[:, slot], psy[:], 1 / (HS * WS),
                                             b2_bc[:, bass.DynSlice(e, 1), :].broadcast_to([P, 2, D]),
                                             ALU.mult, ALU.add).then_inc(y_read, 1)
                if nxt:
                    do_rec_hi(st, -1)
                if st.at(-3, GRAPHS):
                    do_aggr(st, -3)
                if nxt:
                    do_rec_lo(st, -1)
                if yt:
                    dve.wait_ge(old_in[slot], st.val(off, 2, 32, 32))
                    dve.wait_ge(y_read, st.val(off, plus=1))
                    for h in range(2):
                        ins = dve.scalar_tensor_tensor(res[:, slot, h], res[:, slot, h],
                                                       wsel[:, st.slot(off, 4), h:h + 1], old[:, slot, h],
                                                       ALU.mult, ALU.add)
                    ins.then_inc(res_done, 1)
                if st.reg is None and 1 <= st.first <= 2 * E and 2 * st.first - 1 not in lo_by_pool:
                    k = 2 * st.first - 1
                    dve.wait_ge(w_hi, k + 1)
                    dve.tensor_tensor(w_half(k, 1), stage[:, k % 4, :], w_half(k, 0),
                                      ALU.subtract).then_inc(w_lo_dve, 1)
                off = LAG
                if st.at(off, NF):
                    par = st.slot(off, 2)
                    for q in range(FC // 2):
                        if q == 2:
                            routing_between(st)
                        dve.wait_ge(h_hi, st.val(off, 1, FC // 2, q + 1))
                        cols = slice(q * 2 * SLOTS, (q + 1) * 2 * SLOTS)
                        dve.scalar_tensor_tensor(hidden[:, par, 1, cols], h32[:, q % 2, :], HS,
                                                 hidden[:, par, 0, cols], ALU.mult, ALU.subtract).then_inc(h_done, 1)
                else:
                    routing_between(st)
                off = LAG - 1
                if st.at(off, NF):
                    slot = st.slot(off, 2)
                    if st.slot(off, 4) == 0:
                        wait_alone(dve, list_done, min_list(st, off))
                    e = load_expert(dve, st, off)
                    dve.wait_ge(rows_in[slot], st.val(off, 2, 16, 16))
                    dve.tensor_copy(tok[:, st.slot(off, 4), :][:, :, None],
                                    rows[:, slot, :, COL_TOK:ROW].bitcast(I32))
                    dve.tensor_copy(wsel[:, st.slot(off, 4), :][:, :, None],
                                    rows[:, slot, :, COL_W:COL_TOK].bitcast(F32)[:, :, bass.DynSlice(e, 1)]
                                    ).then_inc(meta_done, 1)
                if st.at(0, GRAPHS):
                    dve.wait_ge(gnn_done, st.val(0, plus=1))
                    dve.tensor_reduce(amax[:, 0:1], ps_gnn, AX.X, ALU.max)
                    dve.tensor_reduce(lg[:, st.slot(0, GROUP), :], ps_lg.rearrange("p (k e) -> p e k", k=2), AX.X,
                                      ALU.add).then_inc(amax_done, 1)
                    dve.wait_ge(amax_done, st.val(0, plus=1))
                    dve.tensor_scalar(amax[:, 1:2], amax[:, 0:1], gb_col[:, 0:1], 0.0,
                                      ALU.add, ALU.max).then_inc(amax_mid, 1)
                    dve.wait_ge(amax_mid, st.val(0, plus=1))
                    slot = st.slot(0, 8)
                    dve.scalar_tensor_tensor(xin[:, slot, :], amax[:, 1:2].broadcast_to([P, D]), 1 / (XS * WS),
                                             xin[:, slot, :], ALU.mult, ALU.add).then_inc(init_done, 1)
                routing(st)

            steps(dve, body)

        @block.tensor
        def _(pe):
            pe.wait_ge(const_in, 16 * 6)
            pe.wait_ge(pool_set, 2)
            pe.transpose(ps1[0][:, 0:P], adj_in[:], identf[:])
            pe.transpose(ps1[1][:, 0:E * FC], h32[0:E * FC, 0, 0:P], identf[0:E * FC, 0:E * FC]).then_inc(pe_set, 1)
            pe.wait_ge(dve_set, 2)

            def weight(e, part, col, n):
                return w_all[:, bass.DynSlice(e, 1), part, col:col + n].rearrange("p e c -> p (e c)")

            def products(psum, parts):
                for n, (a, b) in enumerate(parts):
                    ins = pe.matmul(psum, a, b, start=n == 0, stop=n == len(parts) - 1)
                return ins

            def routing(st):
                part = st.i % GROUP
                if part == 0 and st.at(GROUP, GRAPHS):
                    pe.wait_ge(chosen_done, st.val(GROUP, GROUP, 1, 1))
                    if st.later(GROUP, GROUP):
                        pe.wait_ge(pos_read, st.val(GROUP, GROUP))
                    pe.matmul(ps_pos, before[:], chosen[:], start=True, stop=False)
                    for k in range(GROUP):
                        ins = pe.matmul(ps_pos[:, k + 1:, :], ones[:],
                                        chosen[:, k:k + 1, :].broadcast_to([P, GROUP - k, E]),
                                        start=False, stop=k == GROUP - 1)
                    ins.then_inc(pos_done, 1)
                if part == 1 and st.at(GROUP + 1, GRAPHS):
                    wait_alone(pe, new_tiles, st.val(GROUP + 1, GROUP, 1, 1))
                    first_entries()
                if part == 3 and st.at(GROUP + 3, GRAPHS):
                    wait_alone(pe, entries_done, st.val(GROUP + 3, GROUP, 1, 1))
                    if st.later(GROUP + 3, 3 * GROUP):
                        wait_alone(pe, list_done, st.val(GROUP + 3, GROUP, 1, -2))
                    whole_list()
                if st.reg is None and st.first == GRAPHS + GROUP + 1:
                    pe.wait_ge(new_tiles, NG + 1)
                    first_entries()
                if st.reg is None and st.first == GRAPHS + GROUP + 2:
                    pe.wait_ge(entries_done, NG + 1)
                    pe.wait_ge(list_done, NG - 2)
                    whole_list()

            def first_entries():
                pe.matmul(ps_first, beforef[:], ev[:, 2:3], start=True, stop=False)
                pe.matmul(ps_first, onesf[:], ev[:, 0:1], start=False, stop=True).then_inc(first_done, 1)

            def whole_list():
                pe.matmul(ps_list, ones[0:E, 0:1], entries[:], start=True, stop=True).then_inc(list_psum, 1)

            def body(st):
                if st.at(0, GRAPHS):
                    pe.wait_ge(rec_done, st.val(0, plus=1))
                    if st.later(0, 1):
                        pe.wait_ge(amax_done, st.val(0))
                    for c in range(4):
                        ins = pe.transpose(ps_xta[:, c * P:(c + 1) * P],
                                           rec[:, st.slot(0, 8), c * P:(c + 1) * P].bitcast(F16), ident[:])
                    ins.then_inc(xta_psum, 1)
                off = LAG
                if st.at(off, NF):
                    slot = st.slot(off, 2)
                    if st.slot(off, 4) == 0:
                        pe.wait_ge(list_done, min_list(st, off))
                    if st.reg is None and st.first == off:
                        pe.wait_ge(w_hi, 4 * E)
                        pe.wait_ge(w_lo_pool, len(lo_by_pool))
                        pe.wait_ge(w_lo_dve, 4 * E - len(lo_by_pool))
                    e = load_expert(pe, st, off)
                    pe.wait_ge(xt_done, st.val(off, plus=1))
                    for c in range(FC):
                        if c % 2 == 0 and st.later(off, 1):
                            pe.wait_ge(gelu_done, st.val(off, 1, FC, c + 2 - FC))
                        parts = []
                        for dc in range(DC):
                            xh, xl = (xt[:, slot, k, dc * SLOTS:(dc + 1) * SLOTS] for k in range(2))
                            wh, wl = (weight(e, k, dc * DFF + c * P, P) for k in range(2))
                            parts += [(wh, xh), (wh, xl), (wl, xh)]
                        products(ps1[c // 2][:, c % 2 * SLOTS:(c % 2 + 1) * SLOTS], parts).then_inc(h_psum, 1)
                off = LAG - 1
                if st.at(off, NF):
                    slot = st.slot(off, 2)
                    pe.wait_ge(rows_in[slot], st.val(off, 2, 16, 16))
                    if st.later(off, 1):
                        pe.wait_ge(xt_done, st.val(off))
                    for h in range(2):
                        for c in range(4):
                            ins = pe.transpose(ps_xt[:, c // 2, (c % 2 * 2 + h) * P:(c % 2 * 2 + h + 1) * P],
                                               rows[:, slot, h, c * P:(c + 1) * P].bitcast(F16), ident[:])
                    ins.then_inc(xt_psum, 1)
                routing(st)

                if st.at(0, GRAPHS):
                    pe.wait_ge(xta_done, st.val(0, plus=1))
                    slot = st.slot(0, 8)
                    products(ps_lg,
                             [(xta[:, st.slot(0, 2), c * P:(c + 1) * P], wr16[:, c % 2, :]) for c in range(4)])
                    hi, lo = (rec[:, slot, k * D:(k + 1) * D].bitcast(F16) for k in range(2))
                    products(ps_gnn, [(adj_t[:, 0], hi), (adj_t[:, 0], lo), (adj_t[:, 1], hi)]).then_inc(gnn_done, 1)
                off = LAG + 1
                if st.at(off, NF):
                    slot = st.slot(off, 2)
                    e = load_expert(pe, st, off)
                    if st.later(off, 1):
                        pe.wait_ge(y_read, st.val(off))
                    for c in range(FC):
                        if c % 2 == 0:
                            pe.wait_ge(h_done, st.val(off, 1, FC // 2, c // 2 + 1))
                        wh, wl = (weight(e, 2 + k, c * D, D) for k in range(2))
                        for n, (k, w) in enumerate(((0, wh), (1, wh), (0, wl))):
                            for h in range(2):
                                ins = pe.matmul(psy[:, h, :],
                                                hidden[:, slot, k, c * SLOTS + h * P:c * SLOTS + (h + 1) * P], w,
                                                start=c == 0 and n == 0 and h == 0,
                                                stop=c == FC - 1 and n == 2 and h == 1)
                    ins.then_inc(y_psum, 1)

            steps(pe, body)


_INS = ["x", "adj", "L0_gnn_b", "L0_ffn_Wr", "L0_ffn_br", "L0_ffn_W1", "L0_ffn_b1", "L0_ffn_W2", "L0_ffn_b2"]


def kernel(**inputs):
    import concourse.bacc as bacc
    from concourse.bass_utils import run_bass_kernel_spmd

    nc = bacc.Bacc("TRN2", target_bir_lowering=False, num_devices=1)
    arrays, args = {}, []
    for name in _INS:
        a = np.ascontiguousarray(inputs[name])
        arrays[f"in_{name}"] = a
        args.append(nc.dram_tensor(f"in_{name}", a.shape, mybir.dt.from_np(a.dtype), kind="ExternalInput").ap())
    out = nc.dram_tensor("out", (GRAPHS, NODES, D), F32, kind="ExternalOutput").ap()
    build(nc, *args, out)
    result = run_bass_kernel_spmd(nc, [arrays], core_ids=[0])
    return result.results[0]["out"]
```
